# Optimizing a Trainium2 kernel written in Bass

```python
import numpy as np
import jax
import jax.numpy as jnp

def _softmax(x, axis=-1):
    return jax.nn.softmax(x, axis=axis)

def _gelu(x):
    return jax.nn.gelu(x, approximate=True)

def _silu(x):
    return jax.nn.silu(x)

def _sigmoid(x):
    return jax.nn.sigmoid(x)

def _layernorm(x, axis=-1, eps=1e-05):
    m = jnp.mean(x, axis=axis, keepdims=True)
    v = jnp.var(x, axis=axis, keepdims=True)
    return (x - m) / jnp.sqrt(v + eps)

def _scatter_add(tgt, idx, src, axis=0):
    return tgt.at[idx].add(src)

def _segment_sum(src, seg, n):
    return jax.ops.segment_sum(src, seg, n)
kernel_name = 'mk_adj_resnorm_d4_adj_r2_e5a7fd'

def setup_inputs(seed: int=0):
    np.random.seed(seed)
    _w = jnp.asarray

    def _rec_inputs():
        import jax
        import jax.numpy as jnp
        _gk = jax.random.key(seed)
        x = -0.0005207 + 1.001 * jax.random.normal(jax.random.fold_in(_gk, 1), (16, 512, 128), jnp.float32)
        _a = jax.random.bernoulli(jax.random.fold_in(_gk, 2), 0.015625, (16, 512, 512))
        _a = jnp.logical_or(_a, jnp.eye(512, dtype=bool))
        adj = _a.astype(jnp.int32)
        return (x, adj)
    x, adj = _rec_inputs()

    def _L0_gnn_setup():
        import jax, jax.numpy as jnp
        import numpy as np
        B, N, D, H = (4, 1024, 128, 8)
        HD = D // H
        DFF = 4 * D
        EPS = 1e-05

        def layer_norm(x, gamma, beta):
            mu = jnp.mean(x, axis=-1, keepdims=True)
            var = jnp.mean(jnp.square(x - mu), axis=-1, keepdims=True)
            return (x - mu) * jax.lax.rsqrt(var + EPS) * gamma + beta
        key = jax.random.key(seed)
        ks = jax.random.split(key, 10)
        x = jax.random.normal(ks[0], (B, N, D), dtype=jnp.float32)
        adj = jax.random.randint(ks[1], (B, N, N), 0, 2).astype(jnp.int32)
        idx = jnp.arange(N)
        adj = adj.at[:, idx, idx].set(1)
        gamma1 = 1.0 + 0.02 * jax.random.normal(ks[2], (D,), dtype=jnp.float32)
        beta1 = 0.02 * jax.random.normal(ks[3], (D,), dtype=jnp.float32)
        gamma2 = 1.0 + 0.02 * jax.random.normal(ks[4], (D,), dtype=jnp.float32)
        beta2 = 0.02 * jax.random.normal(ks[5], (D,), dtype=jnp.float32)
        W1 = 0.02 * jax.random.normal(ks[6], (D, DFF), dtype=jnp.float32)
        b1 = 0.01 * jax.random.normal(ks[7], (DFF,), dtype=jnp.float32)
        W2 = 0.02 * jax.random.normal(ks[8], (DFF, D), dtype=jnp.float32)
        b2 = 0.01 * jax.random.normal(ks[9], (D,), dtype=jnp.float32)
        return {'x': x, 'adj_matrix': adj, 'gamma1': gamma1, 'beta1': beta1, 'gamma2': gamma2, 'beta2': beta2, 'W1': W1, 'b1': b1, 'W2': W2, 'b2': b2}
    _L0_gnn_all = _L0_gnn_setup()
    _L0_gnn_in = {k: v for k, v in _L0_gnn_all.items() if k in ('gamma1', 'beta1', 'gamma2', 'beta2', 'W1', 'b1', 'W2', 'b2')}
    del _L0_gnn_all

    def _L1_gnn_setup():
        import jax, jax.numpy as jnp
        import numpy as np
        B, N, C_IN, H, C_OUT = (8, 512, 128, 4, 128)
        C = C_OUT // H
        ALPHA = 0.2
        NEG_INF = -9000000000000000.0
        key = jax.random.key(seed)
        k1, k2, k3, k4, k5 = jax.random.split(key, 5)
        node_feats = jax.random.normal(k1, (B, N, C_IN), dtype=jnp.float32)
        adj_matrix = jax.random.randint(k2, (B, N, N), 0, 2, dtype=jnp.int32)
        eye = jnp.eye(N, dtype=jnp.int32)[None]
        adj_matrix = jnp.maximum(adj_matrix, eye)

        def xavier(k, shape, fan_in, fan_out, gain=1.414):
            lim = gain * np.sqrt(6.0 / (fan_in + fan_out))
            return jax.random.uniform(k, shape, jnp.float32, -lim, lim)
        W = xavier(k3, (C_OUT, C_IN), C_IN, C_OUT)
        b = jnp.zeros((C_OUT,), dtype=jnp.float32)
        a = xavier(k4, (H, 2 * C), 2 * C, H)
        return {'node_feats': node_feats, 'adj_matrix': adj_matrix, 'W': W, 'b': b, 'a': a}
    _L1_gnn_all = _L1_gnn_setup()
    _L1_gnn_in = {k: v for k, v in _L1_gnn_all.items() if k in ('W', 'b', 'a')}
    del _L1_gnn_all

    def _L2_gnn_setup():
        import jax, jax.numpy as jnp
        import numpy as np
        NEG_INF = -9000000000000000.0
        LEAKY_SLOPE = 0.2
        key = jax.random.key(seed)
        k1, k2, k3, k4, k5, k6 = jax.random.split(key, 6)
        B, N, D = (256, 200, 128)
        hidden = jax.random.normal(k1, (B, N, D), dtype=jnp.float32)
        adj = jax.random.randint(k2, (B, N, N), 0, 5, dtype=jnp.int32)
        a0 = jax.random.normal(k3, (D,), dtype=jnp.float32)
        a1 = jax.random.normal(k4, (D,), dtype=jnp.float32)
        a2 = jax.random.normal(k5, (D,), dtype=jnp.float32)
        a3 = jax.random.normal(k6, (D,), dtype=jnp.float32)
        return {'hidden': hidden, 'adj': adj, 'a0': a0, 'a1': a1, 'a2': a2, 'a3': a3}
    _L2_gnn_all = _L2_gnn_setup()
    _L2_gnn_in = {k: v for k, v in _L2_gnn_all.items() if k in ('a0', 'a1', 'a2', 'a3')}
    del _L2_gnn_all

    def _L3_gnn_setup():
        import jax, jax.numpy as jnp
        import numpy as np
        LEAKY_SLOPE = 0.2
        NEG_INF = -9000000000000000.0

        def _edge_scores(h, a_k):
            e = jnp.einsum('bid,bjd->bij', h * a_k[:, 0], h)
            return jax.nn.leaky_relu(e, negative_slope=LEAKY_SLOPE)
        key = jax.random.key(seed)
        k1, k2, k3, k4, k5, k6 = jax.random.split(key, 6)
        B, N, D = (32, 256, 128)
        hidden = jax.random.normal(k1, (B, N, D), dtype=jnp.float32)
        adj = jax.random.randint(k2, (B, N, N), 0, 5, dtype=jnp.int32)
        a_0 = jax.random.normal(k3, (D, 1), dtype=jnp.float32)
        a_1 = jax.random.normal(k4, (D, 1), dtype=jnp.float32)
        a_2 = jax.random.normal(k5, (D, 1), dtype=jnp.float32)
        a_3 = jax.random.normal(k6, (D, 1), dtype=jnp.float32)
        return {'hidden': hidden, 'adj': adj, 'a_0': a_0, 'a_1': a_1, 'a_2': a_2, 'a_3': a_3}
    _L3_gnn_all = _L3_gnn_setup()
    _L3_gnn_in = {k: v for k, v in _L3_gnn_all.items() if k in ('a_0', 'a_1', 'a_2', 'a_3')}
    del _L3_gnn_all
    return {'x': x, 'adj': adj, 'L0_gnn_gamma1': _L0_gnn_in['gamma1'], 'L0_gnn_beta1': _L0_gnn_in['beta1'], 'L0_gnn_gamma2': _L0_gnn_in['gamma2'], 'L0_gnn_beta2': _L0_gnn_in['beta2'], 'L0_gnn_W1': _L0_gnn_in['W1'], 'L0_gnn_b1': _L0_gnn_in['b1'], 'L0_gnn_W2': _L0_gnn_in['W2'], 'L0_gnn_b2': _L0_gnn_in['b2'], 'L1_gnn_W': _L1_gnn_in['W'], 'L1_gnn_b': _L1_gnn_in['b'], 'L1_gnn_a': _L1_gnn_in['a'], 'L2_gnn_a0': _L2_gnn_in['a0'], 'L2_gnn_a1': _L2_gnn_in['a1'], 'L2_gnn_a2': _L2_gnn_in['a2'], 'L2_gnn_a3': _L2_gnn_in['a3'], 'L3_gnn_a_0': _L3_gnn_in['a_0'], 'L3_gnn_a_1': _L3_gnn_in['a_1'], 'L3_gnn_a_2': _L3_gnn_in['a_2'], 'L3_gnn_a_3': _L3_gnn_in['a_3']}

def reference(x, adj, L0_gnn_gamma1, L0_gnn_beta1, L0_gnn_gamma2, L0_gnn_beta2, L0_gnn_W1, L0_gnn_b1, L0_gnn_W2, L0_gnn_b2, L1_gnn_W, L1_gnn_b, L1_gnn_a, L2_gnn_a0, L2_gnn_a1, L2_gnn_a2, L2_gnn_a3, L3_gnn_a_0, L3_gnn_a_1, L3_gnn_a_2, L3_gnn_a_3):
    import jax
    import jax.numpy as jnp

    def _L0_gnn_ref(x, adj_matrix, gamma1, beta1, gamma2, beta2, W1, b1, W2, b2):
        import jax, jax.numpy as jnp
        import numpy as np
        B, N, D, H = (4, 1024, 128, 8)
        HD = D // H
        DFF = 4 * D
        EPS = 1e-05

        def layer_norm(x, gamma, beta):
            mu = jnp.mean(x, axis=-1, keepdims=True)
            var = jnp.mean(jnp.square(x - mu), axis=-1, keepdims=True)
            return (x - mu) * jax.lax.rsqrt(var + EPS) * gamma + beta
        b_, n_, d_ = x.shape
        normed = layer_norm(x, gamma1, beta1)
        qkv = normed.reshape(b_, n_, H, HD).transpose(0, 2, 1, 3)
        scale = 1.0 / jnp.sqrt(jnp.asarray(HD, dtype=x.dtype))
        scores = jnp.einsum('bhqd,bhkd->bhqk', qkv, qkv) * scale
        mask = adj_matrix[:, None, :, :] > 0
        masked = jnp.where(mask, scores, -jnp.inf)
        attn = jax.nn.softmax(masked, axis=-1)
        out = jnp.einsum('bhqk,bhkd->bhqd', attn, qkv)
        out = out.transpose(0, 2, 1, 3).reshape(b_, n_, d_)
        x = x + out
        y = layer_norm(x, gamma2, beta2)
        mlp = jax.nn.gelu(y @ W1 + b1, approximate=False) @ W2 + b2
        return x + mlp

    def _L1_gnn_ref(node_feats, adj_matrix, W, b, a):
        import jax, jax.numpy as jnp
        import numpy as np
        B, N, C_IN, H, C_OUT = (8, 512, 128, 4, 128)
        C = C_OUT // H
        ALPHA = 0.2
        NEG_INF = -9000000000000000.0
        Bb, Nn, _ = node_feats.shape
        Hh, twoC = a.shape
        Cc = twoC // 2
        h = (node_feats @ W.T + b).reshape(Bb, Nn, Hh, Cc)
        a_src, a_dst = (a[:, :Cc], a[:, Cc:])
        l_src = jnp.einsum('bihc,hc->bih', h, a_src)
        l_dst = jnp.einsum('bjhc,hc->bjh', h, a_dst)
        logits = jax.nn.leaky_relu(l_src[:, :, None, :] + l_dst[:, None, :, :], ALPHA)
        logits = jnp.where(adj_matrix[..., None] == 1, logits, NEG_INF)
        probs = jax.nn.softmax(logits, axis=2)
        out = jnp.einsum('bijh,bjhc->bihc', probs, h)
        return out.reshape(Bb, Nn, Hh * Cc)

    def _L2_gnn_ref(hidden, adj, a0, a1, a2, a3):
        import jax, jax.numpy as jnp
        import numpy as np
        NEG_INF = -9000000000000000.0
        LEAKY_SLOPE = 0.2

        def edge_score(a):
            s = jnp.einsum('bid,bjd->bij', hidden * a, hidden)
            return jax.nn.leaky_relu(s, LEAKY_SLOPE)
        e0, e1, e2, e3 = (edge_score(a0), edge_score(a1), edge_score(a2), edge_score(a3))
        alpha = jnp.where(adj == 1, e0, NEG_INF)
        alpha = jnp.where(adj == 2, e1, alpha)
        alpha = jnp.where(adj == 3, e2, alpha)
        alpha = jnp.where(adj == 4, e3, alpha)
        alpha = jax.nn.softmax(alpha, axis=-1)
        return jnp.matmul(alpha, hidden)

    def _L3_gnn_ref(hidden, adj, a_0, a_1, a_2, a_3):
        import jax, jax.numpy as jnp
        import numpy as np
        LEAKY_SLOPE = 0.2
        NEG_INF = -9000000000000000.0

        def _edge_scores(h, a_k):
            e = jnp.einsum('bid,bjd->bij', h * a_k[:, 0], h)
            return jax.nn.leaky_relu(e, negative_slope=LEAKY_SLOPE)
        h = hidden
        e_0 = _edge_scores(h, a_0)
        e_1 = _edge_scores(h, a_1)
        e_2 = _edge_scores(h, a_2)
        e_3 = _edge_scores(h, a_3)
        scores = jnp.where(adj == 1, e_0, NEG_INF)
        scores = jnp.where(adj == 2, e_1, scores)
        scores = jnp.where(adj == 3, e_2, scores)
        scores = jnp.where(adj == 4, e_3, scores)
        alpha = jax.nn.softmax(scores, axis=-1)
        return jnp.einsum('bij,bjd->bid', alpha, h)
    x = _layernorm(x + _L0_gnn_ref(x, adj, L0_gnn_gamma1, L0_gnn_beta1, L0_gnn_gamma2, L0_gnn_beta2, L0_gnn_W1, L0_gnn_b1, L0_gnn_W2, L0_gnn_b2), axis=-1)
    x = _layernorm(x + _L1_gnn_ref(x, adj, L1_gnn_W, L1_gnn_b, L1_gnn_a), axis=-1)
    x = _layernorm(x + _L2_gnn_ref(x, adj, L2_gnn_a0, L2_gnn_a1, L2_gnn_a2, L2_gnn_a3), axis=-1)
    x = _layernorm(x + _L3_gnn_ref(x, adj, L3_gnn_a_0, L3_gnn_a_1, L3_gnn_a_2, L3_gnn_a_3), axis=-1)
    return x

_drawn_inputs = setup_inputs


def setup_inputs(seed=0):
    import zlib

    import numpy as np

    out = dict(_drawn_inputs(seed))
    spreads = {'L1_gnn_b': (0.0, 0.1)}
    factors = {'L0_gnn_gamma2': 31.265, 'L0_gnn_beta2': 29.066, 'L0_gnn_b1': 22.919, 'L0_gnn_b2': 3.835}
    for name, (base, spread) in spreads.items():
        noise = np.random.default_rng([zlib.crc32(name.encode()), seed]).standard_normal(out[name].shape)
        drawn = base * np.exp(spread * noise) if base else spread * noise
        out[name] = jnp.asarray(drawn.astype(out[name].dtype))
    for name, factor in factors.items():
        out[name] = (out[name] * factor).astype(out[name].dtype)
    return out
```

```python
from contextlib import ExitStack

import numpy as np
import concourse.bass as bass
from concourse import mybir

fp32 = mybir.dt.float32
bf16 = mybir.dt.bfloat16
fp16 = mybir.dt.float16
i32 = mybir.dt.int32
ALU = mybir.AluOpType
ACT = mybir.ActivationFunctionType
AX = mybir.AxisListType

B, N, D = 16, 512, 128
P = 128
NT = N // P
H0, H1 = 8, 4
D0, D1 = D // H0, D // H1
FF = 4 * D
FC = FF // P
W0, W1C = 3 * D0 + 1, 3 * D1 + 1
EPS = 1e-5
BIG = -9e15
TERMS_L = "hhhmml"
TERMS_R = "hmlhmh"
K0 = len(TERMS_L) * D0
STACK_LOADS = 2 * len(TERMS_L)
LSTACK_LOADS = 6
CONST_LOADS = 20 + 2 * H1
CONSTS = 13

ORDER = [("A", 0), ("A", 1), ("A", 2), ("A", 3), ("C", 0), ("A", 4), ("A", 5), ("A", 6), ("A", 7),
         ("C", 1), ("B", 0), ("B", 1), ("B", 2), ("B", 3)]
LAG = {"A": 0, "B": 1, "C": 2}
SLOTS = len(ORDER)
LOOP = (3, B - 3)
X_USES = ["yT", "f0", "f1", "f2", "f3", "xT2", "w2", "x1T", "proj", "lsd", "xT3", "qh", "qm", "ql"]
X_LAG = {"xT2": 2, "xT3": 2, "yT": 1, "f0": 1, "f1": 1, "f2": 1, "f3": 1, "w2": 1, "x1T": 1, "proj": 1,
         "lsd": 1, "qh": -1, "qm": -1, "ql": -1}


def present(it, lag):
    return not isinstance(it, int) or 0 <= it - lag < B


def count_before(it, lags):
    if isinstance(it, int):
        return sum(min(max(it - lag, 0), B) for lag in lags)
    return len(lags) * it - sum(lags)


def index_in(it, lags, n):
    before = sum(1 for lag in lags[:n] if present(it, lag))
    return count_before(it, lags) + before


class Unit:
    def __init__(self, it, odd, pos):
        self.kind, self.h = ORDER[pos]
        lags = [LAG[k] for k, _ in ORDER]
        self.b = it - LAG[self.kind]
        self.bp = (odd + LAG[self.kind]) % 2
        self.g = index_in(it, lags, pos)
        self.par = self.g % 2 if isinstance(it, int) else (count_before(2, lags) + pos) % 2
        if self.kind != "A":
            leaky = [LAG[k] for k, _ in ORDER if k != "A"]
            self.leaky = index_in(it, leaky, sum(1 for k, _ in ORDER[:pos] if k != "A"))


def due(count):
    return not isinstance(count, int) or count > 0


def val(eng, count):
    return count if isinstance(count, int) else eng.compute_val(count)


class Steps:

    def __init__(self, sem, per):
        self.sem, self.per = sem, per

    def upto(self, b, k):
        return self.per * b + k


def adj_resnorm_kernel(nc, x, adj, gamma1, beta1, gamma2, beta2, W1, b1, W2, b2, Wl1, WTl1, bl1, al1,
                       a2s, a3s, out):
    ctx = ExitStack()
    with ctx:
        def sb(name, shape, dt=fp32):
            return ctx.enter_context(nc.sbuf_tensor(name, shape, dt))

        def sem(name):
            return ctx.enter_context(nc.semaphore(name))

        def steps(name, per):
            return Steps(sem(name), per)

        identf, identh = sb("identf", [P, P]), sb("identh", [P, P], bf16)
        g1b, be1b, g2b, be2b, b2b, bl1b = (sb(n, [P, D]) for n in ("g1b", "be1b", "g2b", "be2b", "b2b", "bl1b"))
        w1s, w2s, b1c = sb("w1s", [P, FF]), sb("w2s", [P, FC, D]), sb("b1c", [P, FC])
        wl, wlT, blc = sb("wl", [P, D]), sb("wlT", [P, D]), sb("blc", [P, 1])
        head_a = sb("head_a", [P, 2 * H1])
        wa, wab = sb("wa", [P, 2 * H1]), sb("wab", [2 * H1, 1])
        ac = [sb("a2c", [P, 4]), sb("a3c", [P, 4])]
        mhalf = sb("mhalf", [P, NT])
        Y = [sb(f"Y{i}", [P, NT, N]) for i in range(2)]
        Pr = [sb(f"Pr{i}", [P, NT, N]) for i in range(2)]
        PTf = [sb(f"PTf{i}", [P, 2 * N]) for i in range(2)]
        PTh = [t[:, 0:N].bitcast(fp16) for t in PTf]
        PTl = [t[:, N:2 * N].bitcast(fp16) for t in PTf]
        mx = [sb(f"mx{i}", [P, NT]) for i in range(2)]
        negmx = [sb(f"negmx{i}", [P, NT]) for i in range(2)]
        nm = [sb(f"nm{i}", [P, NT]) for i in range(2)]
        xin = [sb(f"xin{i}", [P, NT, D]) for i in range(2)]
        adji = [sb(f"adji{i}", [P, NT, N], i32) for i in range(2)]
        bias0 = [sb(f"bias0{i}", [P, NT, N], bf16) for i in range(2)]
        bias1 = [sb(f"bias1{i}", [P, NT, N], bf16) for i in range(2)]
        stL = [sb(f"stL{i}", [K0, H0, N], bf16) for i in range(2)]
        stR = [sb(f"stR{i}", [K0, H0, N], bf16) for i in range(2)]
        qT = {s: sb(f"qT{s}", [P, N], bf16) for s in "hml"}
        VA = [sb(f"VA{i}", [P, NT, 4, D], bf16) for i in range(2)]
        VB = sb("VB", [P, NT, 4, D], bf16)
        OA = [sb(f"OA{i}", [P, H0, NT, W0]) for i in range(2)]
        OB = sb("OB", [P, H1, NT, W1C])
        OC = sb("OC", [P, NT, D])
        qn = sb("qn", [P, NT, D])
        rdA = sb("rdA", [P, H0, NT])
        xr, yn, yT = sb("xr", [P, NT, D]), sb("yn", [P, NT, D]), sb("yT", [P, N])
        hpre = sb("hpre", [P, FC, N])
        sumx, x1, x1T = sb("sumx", [P, NT, D]), sb("x1", [P, NT, D]), sb("x1T", [P, N])
        hp = sb("hp", [P, NT, D])
        lsd = sb("lsd", [2 * H1, N])
        lpart = {s: sb(f"lp{s}", [2 * H1, N], bf16) for s in "hml"}
        st1L, st1R = sb("st1L", [K0, H1, N], bf16), sb("st1R", [K0, H1, N], bf16)
        cB, rdB, x2 = sb("cB", [P, NT, D]), sb("rdB", [P, H1, NT]), sb("x2", [P, NT, D])
        xT23, xaT = sb("xT23", [P, N]), sb("xaT", [P, N])
        sums, rdC = sb("sums", [P, 2, NT]), sb("rdC", [P, 2, NT])
        x3, xo = sb("x3", [P, NT, D]), sb("xo", [P, NT, D])

        def pb(name, n):
            return ctx.enter_context(nc.psum_tensor(name, [P, n * N], fp32))

        S = [pb("S0", 1), pb("S1", 1)]
        T = [pb("T0", 2), pb("T1", 2)]
        O, X = pb("O", 1), pb("X", 1)
        Xh = X[:, :].bitcast(bf16)[:, 0:N]

        junk, flags = sb("junk", [P, NT, N], bf16), sb("flags", [P, B])
        fmax, ones1, minus1, flag = sb("fmax", [P, 1]), sb("ones1", [P, 1]), sb("minus1", [P, 1]), sb("flag", [1, 1], i32)
        saved = nc.dram_tensor("layer1_result", (B, N, D), fp32, kind="Internal").ap()

        parts_dram = nc.dram_tensor("query_parts", (2, 3, P, N), bf16, kind="Internal").ap()

        s_score = sem("s_score")
        s_read = sem("s_read")
        s_neg = sem("s_neg")
        s_leak = sem("s_leak")
        s_exp = sem("s_exp")
        s_tr = sem("s_tr")
        s_hi = sem("s_hi")
        s_lo = sem("s_lo")
        s_pv = sem("s_pv")
        s_oev = sem("s_oev")
        s_x = sem("s_x")
        s_xfree = sem("s_xfree")
        s_adj, s_xin = sem("s_adj"), sem("s_xin")
        s_cload, s_part, s_stack, s_lstack, s_out = sem("s_cload"), sem("s_part"), sem("s_stack"), sem("s_lstack"), sem("s_out")
        s_saved = sem("s_saved")
        s_looked = sem("s_looked")
        s_flag = sem("s_flag")
        s_const = sem("s_const")
        s_cv = sem("s_cv")
        s_cp = sem("s_cp")
        b0_done, b1_done = steps("b0_done", 1), steps("b1_done", 1)
        q_v = steps("q_v", 7)
        cA_v, cA_r = steps("cA_v", 4), steps("cA_r", 1)
        y_v = steps("y_v", 2)
        gelu_v = steps("gelu_v", 1)
        sum_v = steps("sum_v", 2)
        lp_v = steps("lp_v", 5)
        vb_v = steps("vb_v", 5)
        cB_v, cB_r = steps("cB_v", 4), steps("cB_r", 1)
        xaT_v = [steps("xaT2_v", 1), steps("xaT3_v", 1)]
        oc_r = [steps("oc2_r", 1), steps("oc3_r", 1)]
        oc_v = [steps("oc2_v", NT), steps("oc3_v", NT)]

        g_pe, g_act, g_dve = steps("g_pe", 3 + NT), steps("g_act", 4 + NT), steps("g_dve", 4 + 12 * NT + 1 + NT)
        s_gload = sem("s_gload")

        class Norm:

            def __init__(self, name):
                self.st, self.mv = sb(name + "_st", [P, NT, 6]), sb(name + "_mv", [P, NT, 2])
                self.ve, self.rs = sb(name + "_ve", [P, NT]), sb(name + "_rs", [P, NT])
                self.stat = steps(name + "_stat", 2 * NT)
                self.root = steps(name + "_root", 2)
                self.done = steps(name + "_done", NT)

            def stats(self, dve, b, src):
                if due(n := self.root.upto(b, 0)):
                    dve.wait_ge(self.root.sem, n)
                for t in range(NT):
                    dve.bn_stats(self.st[:, t, :], src[:, t, :]).then_inc(self.stat.sem, 1)
                for t in range(NT):
                    n = val(dve, self.stat.upto(b, t + 1))
                    dve.wait_ge(s_const, 1)
                    dve.wait_ge(self.stat.sem, n)
                    dve.bn_aggr(self.mv[:, t, :], self.st[:, t, :]).then_inc(self.stat.sem, 1)

            def roots(self, pool, b):
                ready, free = val(pool, self.stat.upto(b, 2 * NT)), val(pool, self.done.upto(b, 0))
                pool.wait_ge(s_const, 1)
                pool.wait_ge(self.stat.sem, ready)
                if due(free):
                    pool.wait_ge(self.done.sem, free)
                pool.tensor_scalar(self.ve[:, :], self.mv[:, :, 1], EPS, None, ALU.add).then_inc(self.root.sem, 1)
                pool.wait_ge(self.root.sem, self.root.upto(b, 1))
                pool.tensor_tensor(self.rs[:, :], self.ve[:, :], mhalf[:, :], ALU.pow).then_inc(self.root.sem, 1)

            def scale(self, dve, b, src, dst):
                dve.wait_ge(self.root.sem, self.root.upto(b, 2))
                for t in range(NT):
                    dve.tensor_scalar(dst[:, t, :], src[:, t, :], self.mv[:, t, 0:1], self.rs[:, t:t + 1],
                                      ALU.subtract, ALU.mult).then_inc(self.done.sem, 1)

        ln1, ln2, lnf, ln_x2, ln_x3, ln_out, ln_g = (
            Norm(name) for name in ("ln1", "ln2", "lnf", "ln_x2", "ln_x3", "ln_out", "ln_g"))

        ctx.enter_context(nc.allow_non_contiguous_dma(reason="columns of a few hundred constants, once"))
        block = ctx.enter_context(nc.Block())

        def general(eng, program, end=None):
            eng.wait_ge(s_flag, 4)
            raised = eng.value_load(flag[0:1, 0:1], min_val=0, max_val=1)
            with eng.If(raised > 0):
                with eng.Fori(0, B) as b:
                    program(b)
                if end:
                    end()

        LAGS = [LAG[k] for k, _ in ORDER]
        POS = {u: p for p, u in enumerate(ORDER)}

        def g_of(kind, h, b):
            return index_in(b + LAG[kind], LAGS, POS[(kind, h)])

        def after(kind, h, b):
            return g_of(kind, h, b) + 1 if not isinstance(b, int) or b >= 0 else 0

        def x_index(name, b):
            lags = [X_LAG[n] for n in X_USES]
            return index_in(b + X_LAG[name], lags, X_USES.index(name))

        def previous(count, b):
            return count if not isinstance(b, int) or b >= 1 else 0

        def run_iterations(eng, half_slot):
            def iteration(it, odd, units):
                for p in range(SLOTS):
                    unit = Unit(it, odd, p) if present(it, LAG[ORDER[p][0]]) else None
                    units = [unit] + units[:3]
                    half_slot(it, odd, p, *units)
                    half_slot(it, odd, p + 0.5, *units)
                return units

            def last_units(it, odd):
                return [Unit(it, odd, SLOTS - 1 - k) for k in range(3)]

            units = [None] * 3
            for it in range(-1, LOOP[0]):
                units = iteration(it, it % 2, units)
            with eng.Fori(*LOOP, 2) as it:
                middle = iteration(it, LOOP[0] % 2, last_units(it - 1, (LOOP[0] - 1) % 2))
                iteration(it + 1, (LOOP[0] + 1) % 2, middle)
            units = last_units(LOOP[1] - 1, (LOOP[1] - 1) % 2)
            for it in range(LOOP[1], B + 2):
                units = iteration(it, it % 2, units)

        def tiles(dram, b):
            return dram[bass.ds(b, 1), :, :].rearrange("a (t p) n -> p (a t) n", p=P)

        @block.sync
        def _(sp):
            def load(dst, src):
                sp.dma_start(dst, src).then_inc(s_cload, 16)

            def row(v):
                return v.rearrange("(a n) -> a n", a=1).broadcast_to([P, D])
            for dst, v in ((g1b, gamma1), (be1b, beta1), (g2b, gamma2), (be2b, beta2), (b2b, b2), (bl1b, bl1)):
                load(dst[:, :], row(v))
            load(w1s[:, :], W1)
            load(w2s[:, :, :], W2.rearrange("(c p) n -> p c n", p=P))
            load(b1c[:, :], b1.rearrange("(c p) -> p c", p=P))
            load(wl[:, :], Wl1)
            load(wlT[:, :], WTl1)
            load(blc[:, :], bl1.rearrange("(p a) -> p a", a=1))
            for c, vs in ((ac[0], a2s), (ac[1], a3s)):
                for k in range(4):
                    load(c[:, k:k + 1], vs[k])
            sp.wait_ge(s_const, 2)
            for h in range(H1):
                for k in range(2):
                    load(head_a[D1 * h:D1 * (h + 1), H1 * k + h:H1 * k + h + 1],
                         al1[h:h + 1, D1 * k:D1 * (k + 1)].rearrange("a p -> p a"))

            def load_adj(b, bp):
                used, looked = val(sp, b1_done.upto(b - 1, 0)), val(sp, b - 1)
                if due(used):
                    sp.wait_ge(b1_done.sem, used)
                if due(looked):
                    sp.wait_ge(s_looked, looked)
                sp.dma_start(adji[bp][:, :, :], tiles(adj, b)).then_inc(s_adj, 16)

            def load_x(b, bp):
                if due(n := sum_v.upto(b - 1, 0)):
                    sp.wait_ge(sum_v.sem, n)
                sp.dma_start(xin[bp][:, :, :], tiles(x, b)).then_inc(s_xin, 16)

            def keep_part(k, b, bp):
                evacuated, read_back = val(sp, x_index("q" + "hml"[k], b) + 1), val(sp, 16 * STACK_LOADS * (b - 1))
                sp.wait_ge(s_xfree, evacuated)
                if due(read_back):
                    sp.wait_ge(s_stack, read_back)
                sp.dma_start(parts_dram[bp, k, :, :], qT["hml"[k]][:, :]).then_inc(s_part, 16)

            def stack(b, bp):
                kept, scored = val(sp, 16 * 3 * (b + 1)), val(sp, 4 * after("A", H0 - 1, b - 2))
                sp.wait_ge(s_part, kept)
                if due(scored):
                    sp.wait_ge(s_score, scored)
                part = parts_dram[bp].rearrange("s (h d) n -> s d h n", d=D0)
                for st, terms in ((stL, TERMS_L), (stR, TERMS_R)):
                    for k, s in enumerate(terms):
                        sp.dma_start(st[bp][D0 * k:D0 * (k + 1), :, :], part["hml".index(s)]).then_inc(s_stack, 16)

            def lstack(b, bp):
                split, scored = val(sp, lp_v.upto(b, 5)), val(sp, previous(4 * after("B", H1 - 1, b - 1), b))
                sp.wait_ge(lp_v.sem, split)
                if due(scored):
                    sp.wait_ge(s_score, scored)
                for k, s in enumerate("hml"):
                    sp.dma_start(st1L[k:k + 1, :, :], lpart[s][0:H1, :]).then_inc(s_lstack, 16)
                    sp.dma_start(st1R[3 + k:4 + k, :, :], lpart[s][H1:2 * H1, :]).then_inc(s_lstack, 16)

            def save(b, bp):
                sp.wait_ge(ln_x2.done.sem, ln_x2.done.upto(b, NT))
                sp.dma_start(tiles(saved, b), x2[:, :, :]).then_inc(s_saved, 16)

            def store(b, bp):
                sp.wait_ge(ln_out.done.sem, ln_out.done.upto(b, NT))
                sp.dma_start(tiles(out, b), xo[:, :, :]).then_inc(s_out, 16)

            def half_slot(it, odd, at, *units):
                if present(it, -1):
                    ahead = it + 1, 1 - odd
                    if at == 0:
                        load_adj(*ahead)
                    if at == 5.5:
                        load_x(*ahead)
                    if at in (11, 11.5, 12):
                        keep_part(int(2 * (at - 11)), *ahead)
                    if at == 12.5:
                        stack(*ahead)
                if present(it, 1) and at == 8:
                    lstack(it - 1, 1 - odd)
                if present(it, 2):
                    if at == 5:
                        save(it - 2, odd)
                    if at == 13:
                        store(it - 2, odd)
            run_iterations(sp, half_slot)
            sp.wait_ge(s_out, 16 * B)
            sp.wait_ge(s_saved, 16 * B)

            def general_sp(b):
                sp.wait_ge(s_out, val(sp, 16 * (b + B)))
                sp.dma_start(x2[:, :, :], tiles(saved, b)).then_inc(s_gload, 16)
                sp.dma_start(adji[0][:, :, :], tiles(adj, b)).then_inc(s_gload, 16)
                sp.wait_ge(ln_g.done.sem, NT * (2 * b + 2))
                sp.dma_start(tiles(out, b), xo[:, :, :]).then_inc(s_out, 16)
            general(sp, general_sp, lambda: sp.wait_ge(s_out, 16 * 2 * B))

        @block.gpsimd
        def _(pool):
            pool.memset(identf[:, :], 0.0).then_inc(s_const, 1)
            pool.memset(head_a[:, :], 0.0).then_inc(s_const, 1)
            pool.memset(identh[:, :], 0.0).then_inc(s_const, 1)
            pool.wait_ge(s_const, 3)
            for m in (identf, identh):
                pool.affine_select(out=m[:, :], in_=m[:, :], compare_op=ALU.not_equal, fill=1.0, base=0,
                                   pattern=[[-1, P]], channel_multiplier=1).then_inc(s_const, 1)
            pool.memset(mhalf[:, :], -0.5).then_inc(s_const, 1)
            for st in (st1L, st1R):
                pool.memset(st[:, :, :], 0.0).then_inc(s_const, 1)
            pool.wait_ge(s_const, 8)
            for st in (st1L, st1R):
                pool.memset(st[0:6, :, :], 1.0).then_inc(s_const, 1)
            for v in (VA[0], VA[1], VB):
                pool.memset(v[:, :, 3, :], 1.0).then_inc(s_const, 1)
            pool.wait_ge(s_const, CONSTS)
            pool.wait_ge(s_cload, 16 * CONST_LOADS)

            def make_bias0(b, bp):
                arrived, used = val(pool, 16 * (b + 1)), val(pool, 4 * after("A", H0 - 1, b - 2))
                pool.wait_ge(s_const, 1)
                pool.wait_ge(s_adj, arrived)
                if due(used):
                    pool.wait_ge(s_read, used)
                pool.tensor_scalar(bias0[bp][:, :, :], adji[bp][:, :, :], 0.0, BIG, ALU.is_le,
                                   ALU.mult).then_inc(b0_done.sem, 1)

            def parts(v, b, k, src, part):
                pool.tensor_copy(part(0), src).then_inc(v.sem, 1)
                pool.wait_ge(v.sem, v.upto(b, k + 1))
                pool.tensor_tensor(src, src, part(0), ALU.subtract).then_inc(v.sem, 1)
                n = val(pool, v.upto(b, k + 2))
                pool.wait_ge(s_const, 1)
                pool.wait_ge(v.sem, n)
                pool.tensor_copy(part(1), src).then_inc(v.sem, 1)
                pool.wait_ge(v.sem, v.upto(b, k + 3))
                pool.tensor_tensor(src, src, part(1), ALU.subtract).then_inc(v.sem, 1)
                n = val(pool, v.upto(b, k + 4))
                pool.wait_ge(s_const, 1)
                pool.wait_ge(v.sem, n)
                pool.tensor_copy(part(2), src).then_inc(v.sem, 1)

            def bc(t):
                return t[:, :].rearrange("p (a d) -> p a d", a=1).broadcast_to([P, NT, D])

            def q_parts(b, bp):
                pool.wait_ge(ln1.done.sem, ln1.done.upto(b, NT))
                pool.tensor_tensor(qn[:, :, :], qn[:, :, :], bc(g1b), ALU.mult).then_inc(q_v.sem, 1)
                pool.wait_ge(q_v.sem, q_v.upto(b, 1))
                pool.tensor_tensor(qn[:, :, :], qn[:, :, :], bc(be1b), ALU.add).then_inc(q_v.sem, 1)
                affine, used = val(pool, q_v.upto(b, 2)), val(pool, 2 * after("A", H0 - 1, b - 2))
                pool.wait_ge(s_const, 1)
                pool.wait_ge(q_v.sem, affine)
                if due(used):
                    pool.wait_ge(s_pv, used)
                parts(q_v, b, 2, qn[:, :, :], lambda k: VA[bp][:, :, k, :])

            def combine(v, b, heads, d, src, recips, sums_ready, dst, residual):
                o = lambda k: src[:, :, :, d * k:d * (k + 1)]
                by_head = dst[:, :, :].rearrange("p t (h d) -> p h t d", h=heads)
                pool.tensor_tensor(by_head, o(0), o(1), ALU.add).then_inc(v.sem, 1)
                pool.wait_ge(v.sem, v.upto(b, 1))
                pool.tensor_tensor(by_head, by_head, o(2), ALU.add).then_inc(v.sem, 1)
                pool.wait_ge(v.sem, v.upto(b, 2))
                pool.wait_ge(sums_ready.sem, sums_ready.upto(b, 1))
                over = recips[:, :, :].rearrange("p h (t a) -> p h t a", a=1).broadcast_to([P, heads, NT, d])
                pool.tensor_tensor(by_head, by_head, over, ALU.mult).then_inc(v.sem, 1)
                pool.wait_ge(v.sem, v.upto(b, 3))
                pool.tensor_tensor(dst[:, :, :], dst[:, :, :], residual[:, :, :], ALU.add).then_inc(v.sem, 1)

            def combine_a(b, bp):
                if due(n := ln2.done.upto(b, 0)):
                    pool.wait_ge(ln2.done.sem, n)
                if due(n := previous(x_index("w2", b - 1) + 1, b)):
                    pool.wait_ge(s_xfree, n)
                pool.wait_ge(s_oev, g_of("A", H0 - 1, b) + 1)
                combine(cA_v, b, H0, D0, OA[bp], rdA, cA_r, xr, xin[bp])

            def combine_b(b, bp):
                if due(n := ln_x2.done.upto(b, 0)):
                    pool.wait_ge(ln_x2.done.sem, n)
                pool.wait_ge(s_oev, g_of("B", H1 - 1, b) + 1)
                combine(cB_v, b, H1, D1, OB, rdB, cB_r, cB, x1)

            def y_affine(b, bp):
                pool.wait_ge(ln2.done.sem, ln2.done.upto(b, NT))
                pool.tensor_tensor(yn[:, :, :], yn[:, :, :], bc(g2b), ALU.mult).then_inc(y_v.sem, 1)
                pool.wait_ge(y_v.sem, y_v.upto(b, 1))
                pool.tensor_tensor(yn[:, :, :], yn[:, :, :], bc(be2b), ALU.add).then_inc(y_v.sem, 1)

            def add_up(b, bp):
                pool.wait_ge(s_xfree, x_index("w2", b) + 1)
                pool.tensor_tensor(sumx[:, :, :], sumx[:, :, :], bc(b2b), ALU.add).then_inc(sum_v.sem, 1)
                pool.wait_ge(sum_v.sem, sum_v.upto(b, 1))
                pool.tensor_tensor(sumx[:, :, :], sumx[:, :, :], xin[bp][:, :, :], ALU.add).then_inc(sum_v.sem, 1)

            def l_parts(b, bp):
                rows, free = val(pool, x_index("lsd", b) + 1), val(pool, 16 * LSTACK_LOADS * b)
                pool.wait_ge(s_const, 1)
                pool.wait_ge(s_xfree, rows)
                if due(free):
                    pool.wait_ge(s_lstack, free)
                parts(lp_v, b, 0, lsd[:, :], lambda k: lpart["hml"[k]][:, :])

            def v_parts(b, bp):
                projected, used = val(pool, x_index("proj", b) + 1), val(pool, 2 * after("B", H1 - 1, b - 1))
                pool.wait_ge(s_const, 1)
                pool.wait_ge(s_xfree, projected)
                if due(used):
                    pool.wait_ge(s_pv, used)
                parts(vb_v, b, 0, hp[:, :, :], lambda k: VB[:, :, k, :])

            def half_slot(it, odd, at, *units):
                if present(it, 2):
                    if at == 2:
                        combine_b(it - 2, odd)
                    if at == 3:
                        ln_x2.roots(pool, it - 2)
                    if at == 7:
                        ln_x3.roots(pool, it - 2)
                if present(it, 1):
                    if at == 4.5:
                        add_up(it - 1, 1 - odd)
                    if at == 5:
                        lnf.roots(pool, it - 1)
                    if at == 7.5:
                        l_parts(it - 1, 1 - odd)
                        v_parts(it - 1, 1 - odd)
                if present(it, -1):
                    if at == 1.5:
                        make_bias0(it + 1, 1 - odd)
                    if at == 6:
                        ln1.roots(pool, it + 1)
                    if at == 8.5:
                        q_parts(it + 1, 1 - odd)
                if present(it, 0) and at == 11:
                    combine_a(it, odd)
                if present(it, 2) and at == 12:
                    ln_out.roots(pool, it - 2)
                if present(it, 0):
                    if at == 12:
                        ln2.roots(pool, it)
                    if at == 12.5:
                        y_affine(it, odd)
            run_iterations(pool, half_slot)

            def general_pool(b):
                for k in range(2):
                    n = 2 * b + k
                    ready = val(pool, ln_g.stat.upto(n, 2 * NT))
                    pool.wait_ge(s_const, 1)
                    pool.wait_ge(ln_g.stat.sem, ready)
                    pool.tensor_scalar(ln_g.ve[:, :], ln_g.mv[:, :, 1], EPS, None, ALU.add).then_inc(ln_g.root.sem, 1)
                    pool.wait_ge(ln_g.root.sem, ln_g.root.upto(n, 1))
                    pool.tensor_tensor(ln_g.rs[:, :], ln_g.ve[:, :], mhalf[:, :], ALU.pow).then_inc(ln_g.root.sem, 1)
            general(pool, general_pool)

        @block.scalar
        def _(act):
            act.wait_ge(s_cv, 4)

            def exps(u):
                if u.kind == "A":
                    act.wait_ge(s_neg, u.g + 1)
                else:
                    act.wait_ge(s_leak, u.leaky + 1)
                if due(n := 2 * (u.g - 1)):
                    act.wait_ge(s_tr, n)
                if u.kind == "C" and due(n := oc_r[u.h].upto(u.b, 0)):
                    act.wait_ge(oc_r[u.h].sem, n)
                for i in range(NT):
                    more = {"accum_out": sums[:, u.h, i:i + 1]} if u.kind == "C" else {}
                    act.activation(Pr[u.par][:, i, :], Y[u.par][:, i, :], ACT.Exp, bias=nm[u.par][:, i:i + 1],
                                   scale=D0 ** -0.5 if u.kind == "A" else 1.0, **more).then_inc(s_exp, 1)

            def high(u, half):
                act.wait_ge(s_tr, 2 * u.g + half + 1)
                if due(n := 2 * (u.g - 1) + half + 1):
                    act.wait_ge(s_pv, n)
                if u.kind == "C":
                    act.activation(PTf[half][:, 0:N], T[half][:, 0:N], ACT.Copy).then_inc(s_hi, 1)
                else:
                    act.activation(PTh[half], T[half][:, :], ACT.Copy).then_inc(s_hi, 1)

            def result(u):
                if u.kind == "A":
                    if due(n := cA_v.upto(u.b - 1, 0)):
                        act.wait_ge(cA_v.sem, n)
                    dst, src = OA[u.bp][:, u.h, :, :], O[:, 0:NT * 4 * D0].rearrange("p (t c) -> p t c", t=NT)[:, :, 0:W0]
                elif u.kind == "B":
                    if due(n := cB_v.upto(u.b, 0)):
                        act.wait_ge(cB_v.sem, n)
                    dst, src = OB[:, u.h, :, :], O[:, 0:NT * 4 * D1].rearrange("p (t c) -> p t c", t=NT)[:, :, 0:W1C]
                else:
                    norm = ln_x3 if u.h else ln_out
                    if due(n := norm.done.upto(u.b + u.h, 0)):
                        act.wait_ge(norm.done.sem, n)
                    dst, src = OC[:, :, :], O[:, :].rearrange("p (t c) -> p t c", t=NT)
                act.wait_ge(s_pv, 2 * u.g + 2)
                act.activation(dst, src, ACT.Copy).then_inc(s_oev, 1)

            def evacuate(name, b, dst, src):
                act.wait_ge(s_x, x_index(name, b) + 1)
                act.activation(dst, src, ACT.Copy).then_inc(s_xfree, 1)

            def gelu(b):
                act.wait_ge(s_xfree, x_index("f3", b) + 1)
                act.activation(hpre[:, :, :], hpre[:, :, :], ACT.Gelu).then_inc(gelu_v.sem, 1)

            def look(b, bp):
                act.wait_ge(s_adj, 16 * (b + 1))
                act.activation(junk[:, :, :], adji[bp][:, :, :], ACT.Relu, bias=minus1[:, 0:1],
                               accum_out=flags[:, bass.ds(b, 1)]).then_inc(s_looked, 1)

            def half_slot(it, odd, at, now, back1, back2, back3):
                if present(it, 1):
                    if at == 0:
                        evacuate("yT", it - 1, yT[:, :], X[:, :])
                    if at == 3.5:
                        gelu(it - 1)
                    if at == 6:
                        evacuate("x1T", it - 1, x1T[:, :], X[:, :])
                if present(it, 2):
                    if at == 4:
                        evacuate("xT2", it - 2, xT23[:, :], X[:, :])
                    if at == 8.5:
                        evacuate("xT3", it - 2, xT23[:, :], X[:, :])
                if present(it, -1):
                    if at == 3:
                        look(it + 1, 1 - odd)
                    if at in (11, 11.5, 12):
                        k = int(2 * (at - 11))
                        if due(n := 16 * (3 * it + 3)):
                            act.wait_ge(s_part, n)
                        evacuate("q" + "hml"[k], it + 1, qT["hml"[k]][:, :], Xh)
                if at == int(at):
                    if back3:
                        result(back3)
                    if back1:
                        exps(back1)
                elif back1:
                    high(back1, 0)
                    high(back1, 1)
            run_iterations(act, half_slot)

            def general_act(b):
                for k in range(2):
                    n = 2 * b + k
                    act.wait_ge(g_pe.sem, g_pe.upto(n, 1))
                    act.activation(xT23[:, :], X[:, :], ACT.Copy).then_inc(g_act.sem, 1)
                    act.wait_ge(g_dve.sem, g_dve.upto(n, 4 + 12 * NT))
                    for i in range(NT):
                        act.activation(Pr[0][:, i, :], Y[0][:, i, :], ACT.Exp, bias=nm[0][:, i:i + 1],
                                       accum_out=sums[:, 0, i:i + 1]).then_inc(g_act.sem, 1)
                    act.wait_ge(g_pe.sem, g_pe.upto(n, 2 + NT))
                    for half in range(2):
                        act.activation(Y[1][:, 2 * half:2 * half + 2, :], T[half][:, :].rearrange("p (i n) -> p i n", i=2),
                                       ACT.Copy).then_inc(g_act.sem, 1)
                    act.wait_ge(g_pe.sem, g_pe.upto(n, 3 + NT))
                    act.activation(OC[:, :, :], O[:, :].rearrange("p (t c) -> p t c", t=NT), ACT.Copy).then_inc(g_act.sem, 1)
            general(act, general_act)

        @block.vector
        def _(dve):
            dve.wait_ge(s_cp, 2)
            dve.tensor_copy(wa[:, :], O[:, 0:2 * H1]).then_inc(s_cv, 1)
            dve.tensor_copy(wab[:, :], X[0:2 * H1, 0:1]).then_inc(s_cv, 1)
            dve.wait_ge(s_const, CONSTS)
            dve.wait_ge(s_cload, 16 * CONST_LOADS)
            dve.sem_inc(s_cv, 1)
            dve.memset(minus1[:, :], -1.0).then_inc(s_cv, 1)
            dve.memset(ones1[:, :], 1.0).then_inc(s_flag, 1)

            def mask(u, i):
                scored, left = val(dve, 4 * u.g + i + 1), val(dve, 4 * (u.g - 1))
                bias, made = (bias0, b0_done) if u.kind == "A" else (bias1, b1_done)
                biased = val(dve, made.upto(u.b, 1))
                dve.wait_ge(s_const, 1)
                dve.wait_ge(s_score, scored)
                if i == 0:
                    if due(left):
                        dve.wait_ge(s_exp, left)
                    dve.wait_ge(made.sem, biased)
                dve.tensor_tensor_reduce(out=Y[u.par][:, i, :], in0=S[i % 2][:, :], in1=bias[u.bp][:, i, :], scale=1.0,
                                         scalar=-3e38, op0=ALU.add, op1=ALU.max,
                                         accum_out=mx[u.par][:, i:i + 1]).then_inc(s_read, 1)

            def maxima(u):
                p = u.par
                dve.wait_ge(s_read, 4 * u.g + 4)
                if u.kind == "A":
                    dve.tensor_scalar(nm[p][:, :], mx[p][:, :], -D0 ** -0.5, None, ALU.mult).then_inc(s_neg, 1)
                    return
                dve.tensor_scalar(negmx[p][:, :], mx[p][:, :], -1.0, None, ALU.mult).then_inc(s_neg, 1)
                dve.scalar_tensor_tensor(out=Y[p][:, :, :], in0=Y[p][:, :, :], scalar=0.2, in1=Y[p][:, :, :],
                                         op0=ALU.mult, op1=ALU.max)
                dve.wait_ge(s_neg, u.g + 1)
                dve.scalar_tensor_tensor(out=nm[p][:, :], in0=mx[p][:, :], scalar=-0.2, in1=negmx[p][:, :],
                                         op0=ALU.mult, op1=ALU.min).then_inc(s_leak, 1)

            def low(u, half):
                if due(n := 2 * (u.g - 1) + half + 1):
                    dve.wait_ge(s_pv, n)
                if u.kind == "C":
                    dve.wait_ge(s_tr, 2 * u.g + half + 1)
                    dve.tensor_copy(PTf[half][:, N:2 * N], T[half][:, N:2 * N]).then_inc(s_lo, 1)
                else:
                    dve.wait_ge(s_hi, 2 * u.g + half + 1)
                    dve.tensor_tensor(PTl[half], T[half][:, :], PTh[half], ALU.subtract).then_inc(s_lo, 1)

            def make_bias1(b, bp):
                dve.wait_ge(s_adj, 16 * (b + 1))
                dve.wait_ge(b0_done.sem, b0_done.upto(b, 1))
                dve.tensor_scalar(bias1[bp][:, :, :], adji[bp][:, :, :], 1.0, BIG, ALU.not_equal,
                                  ALU.mult).then_inc(b1_done.sem, 1)

            def invert_sums(done, b, last, dst, src):
                dve.wait_ge(s_oev, last + 1)
                dve.reciprocal(dst[:, :, :], src).then_inc(done.sem, 1)

            def ff_bias(b, c):
                dve.wait_ge(s_x, x_index(f"f{c}", b) + 1)
                dve.tensor_scalar(hpre[:, c, :], X[:, :], b1c[:, c:c + 1], None, ALU.add).then_inc(s_xfree, 1)

            def mlp_residual(b):
                if due(n := lnf.done.upto(b, 0)):
                    dve.wait_ge(lnf.done.sem, n)
                dve.wait_ge(s_x, x_index("w2", b) + 1)
                dve.tensor_tensor(sumx[:, :, :], X[:, :].rearrange("p (t d) -> p t d", t=NT), xr[:, :, :],
                                  ALU.add).then_inc(s_xfree, 1)

            def projected(b):
                if due(n := vb_v.upto(b, 0)):
                    dve.wait_ge(vb_v.sem, n)
                dve.wait_ge(s_x, x_index("proj", b) + 1)
                bias = bl1b[:, :].rearrange("p (a d) -> p a d", a=1).broadcast_to([P, NT, D])
                dve.tensor_tensor(hp[:, :, :], X[:, :].rearrange("p (t d) -> p t d", t=NT), bias,
                                  ALU.add).then_inc(s_xfree, 1)

            def logits(b):
                if due(n := lp_v.upto(b, 0)):
                    dve.wait_ge(lp_v.sem, n)
                dve.wait_ge(s_x, x_index("lsd", b) + 1)
                dve.tensor_scalar(lsd[:, :], X[0:2 * H1, :], wab[:, 0:1], None, ALU.add).then_inc(s_xfree, 1)

            def scaled(k, b):
                dve.wait_ge(s_xfree, x_index(f"xT{k + 2}", b) + 1)
                dve.tensor_scalar(xaT[:, :], xT23[:, :], ac[k][:, 0:1], None, ALU.mult).then_inc(xaT_v[k].sem, 1)

            def attend(k, xprev, b):
                dve.wait_ge(s_oev, g_of("C", k, b) + 1)
                dve.reciprocal(rdC[:, k, :], sums[:, k, :]).then_inc(oc_r[k].sem, 1)
                dve.wait_ge(oc_r[k].sem, oc_r[k].upto(b, 1))
                for t in range(NT):
                    dve.scalar_tensor_tensor(out=OC[:, t, :], in0=OC[:, t, :], scalar=rdC[:, k, t:t + 1],
                                             in1=xprev[:, t, :], op0=ALU.mult, op1=ALU.add).then_inc(oc_v[k].sem, 1)

            def half_slot(it, odd, at, now, back1, back2, back3):
                if present(it, 2):
                    b = it - 2
                    if at == 2:
                        invert_sums(cB_r, b, g_of("B", H1 - 1, b), rdB, OB[:, :, :, W1C - 1])
                    if at == 3:
                        dve.wait_ge(cB_v.sem, cB_v.upto(b, 4))
                        ln_x2.stats(dve, b, cB)
                    if at == 3.5:
                        if due(n := ln_x3.stat.upto(b, 0)):
                            dve.wait_ge(ln_x3.stat.sem, n)
                        if due(n := 16 * b):
                            dve.wait_ge(s_saved, n)
                        ln_x2.scale(dve, b, cB, x2)
                    if at == 4:
                        scaled(0, b)
                    if at == 7:
                        attend(0, x2, b)
                        dve.wait_ge(oc_v[0].sem, oc_v[0].upto(b, NT))
                        ln_x3.stats(dve, b, OC)
                    if at == 7.5:
                        ln_x3.scale(dve, b, OC, x3)
                    if at == 8.5:
                        scaled(1, b)
                if present(it, 1):
                    b = it - 1
                    if at in (1.5, 2, 2.5, 3):
                        ff_bias(b, int(2 * (at - 1.5)))
                    if at == 4.5:
                        mlp_residual(b)
                    if at == 5:
                        dve.wait_ge(sum_v.sem, sum_v.upto(b, 2))
                        lnf.stats(dve, b, sumx)
                    if at == 5.5:
                        if due(n := cB_v.upto(b, 0)):
                            dve.wait_ge(cB_v.sem, n)
                        if due(n := previous(x_index("x1T", b - 1) + 1, b)):
                            dve.wait_ge(s_x, n)
                        lnf.scale(dve, b, sumx, x1)
                    if at == 7:
                        projected(b)
                    if at == 7.5:
                        logits(b)
                if present(it, -1):
                    b = it + 1
                    if at == 6:
                        dve.wait_ge(s_xin, 16 * (b + 1))
                        ln1.stats(dve, b, xin[1 - odd])
                    if at == 6.5:
                        if due(n := q_v.upto(b, 0)):
                            dve.wait_ge(q_v.sem, n)
                        ln1.scale(dve, b, xin[1 - odd], qn)
                if present(it, 0):
                    if at == 10:
                        make_bias1(it, odd)
                    if at == 11:
                        invert_sums(cA_r, it, g_of("A", H0 - 1, it), rdA, OA[odd][:, :, :, W0 - 1])
                    if at == 12:
                        dve.wait_ge(cA_v.sem, cA_v.upto(it, 4))
                        ln2.stats(dve, it, xr)
                if present(it, 2) and at == 12:
                    attend(1, x3, it - 2)
                    dve.wait_ge(oc_v[1].sem, oc_v[1].upto(it - 2, NT))
                    ln_out.stats(dve, it - 2, OC)
                if present(it, 0) and at == 12.5:
                    if due(n := previous(x_index("yT", it - 1) + 1, it)):
                        dve.wait_ge(s_x, n)
                    ln2.scale(dve, it, xr, yn)
                if present(it, 2) and at == 12.5:
                    if due(n := 16 * (it - 2)):
                        dve.wait_ge(s_out, n)
                    ln_out.scale(dve, it - 2, OC, xo)
                if at == int(at):
                    if now:
                        mask(now, 0)
                    if back2:
                        low(back2, 0)
                    if now:
                        mask(now, 1)
                    if back2:
                        low(back2, 1)
                elif now:
                    mask(now, 2)
                    mask(now, 3)
                    maxima(now)
            run_iterations(dve, half_slot)

            dve.wait_ge(s_looked, B)
            dve.tensor_reduce(fmax[:, :], flags[:, :], AX.X, ALU.max).then_inc(s_flag, 1)
            dve.wait_ge(s_flag, 3)
            dve.tensor_scalar(flag[:, :], X[0:1, 0:1], 0.0, None, ALU.is_gt).then_inc(s_flag, 1)

            def general_dve(b):
                masks = [hpre[:, m, :].bitcast(i32) for m in range(4)]
                for k in range(2):
                    n = 2 * b + k
                    xk = x2 if k == 0 else x3
                    dve.wait_ge(g_act.sem, g_act.upto(n, 1))
                    for m in range(4):
                        dve.tensor_scalar(Pr[1][:, m, :], xT23[:, :], ac[k][:, m:m + 1], None,
                                          ALU.mult).then_inc(g_dve.sem, 1)
                    dve.wait_ge(s_gload, 16 * 2 * (b + 1))
                    for i in range(NT):
                        row = 4 + 12 * i
                        dve.memset(Y[0][:, i, :], BIG).then_inc(g_dve.sem, 1)
                        dve.wait_ge(g_dve.sem, g_dve.upto(n, row + 1))
                        for m in range(4):
                            dve.tensor_scalar(masks[m], adji[0][:, i, :], float(m + 1), None,
                                              ALU.is_equal).then_inc(g_dve.sem, 1)
                        for m in range(4):
                            own, scored = val(dve, g_dve.upto(n, row + 5 + m)), val(dve, g_pe.upto(n, 2 + i))
                            dve.wait_ge(s_const, 1)
                            dve.wait_ge(g_dve.sem, own)
                            dve.wait_ge(g_pe.sem, scored)
                            dve.copy_predicated(Y[0][:, i, :], masks[m],
                                                T[m // 2][:, N * (m % 2):N * (m % 2 + 1)]).then_inc(g_dve.sem, 1)
                        dve.wait_ge(g_dve.sem, g_dve.upto(n, row + 9))
                        dve.scalar_tensor_tensor(out=Y[0][:, i, :], in0=Y[0][:, i, :], scalar=0.2, in1=Y[0][:, i, :],
                                                 op0=ALU.mult, op1=ALU.max).then_inc(g_dve.sem, 1)
                        dve.wait_ge(g_dve.sem, g_dve.upto(n, row + 10))
                        dve.tensor_reduce(mx[0][:, i:i + 1], Y[0][:, i, :], AX.X, ALU.max).then_inc(g_dve.sem, 1)
                        dve.wait_ge(g_dve.sem, g_dve.upto(n, row + 11))
                        dve.tensor_scalar(nm[0][:, i:i + 1], mx[0][:, i:i + 1], -1.0, None, ALU.mult).then_inc(g_dve.sem, 1)
                    end = 4 + 12 * NT
                    dve.wait_ge(g_act.sem, g_act.upto(n, 4 + NT))
                    dve.reciprocal(rdC[:, 0, :], sums[:, 0, :]).then_inc(g_dve.sem, 1)
                    dve.wait_ge(g_dve.sem, g_dve.upto(n, end + 1))
                    for t in range(NT):
                        dve.scalar_tensor_tensor(out=OC[:, t, :], in0=OC[:, t, :], scalar=rdC[:, 0, t:t + 1],
                                                 in1=xk[:, t, :], op0=ALU.mult, op1=ALU.add).then_inc(g_dve.sem, 1)
                    dve.wait_ge(g_dve.sem, g_dve.upto(n, end + 1 + NT))
                    for t in range(NT):
                        dve.bn_stats(ln_g.st[:, t, :], OC[:, t, :]).then_inc(ln_g.stat.sem, 1)
                    for t in range(NT):
                        got = val(dve, ln_g.stat.upto(n, t + 1))
                        dve.wait_ge(s_const, 1)
                        dve.wait_ge(ln_g.stat.sem, got)
                        dve.bn_aggr(ln_g.mv[:, t, :], ln_g.st[:, t, :]).then_inc(ln_g.stat.sem, 1)
                    ln_g.scale(dve, n, OC, x3 if k == 0 else xo)
            general(dve, general_dve)

        @block.tensor
        def _(pe):
            pe.wait_ge(s_cload, 16 * CONST_LOADS)
            pe.wait_ge(s_const, CONSTS)
            pe.matmul(O[:, 0:2 * H1], wl[:, :], head_a[:, :], start=True, stop=True).then_inc(s_cp, 1)
            pe.matmul(X[0:2 * H1, 0:1], head_a[:, :], blc[:, :], start=True, stop=True).then_inc(s_cp, 1)
            pe.wait_ge(s_cv, 2)

            def scores(u, i):
                if due(n := 4 * u.g + i - 1):
                    pe.wait_ge(s_read, n)
                rows = slice(P * i, P * (i + 1))
                if u.kind == "A":
                    if i == 0 and u.h == 0:
                        pe.wait_ge(s_stack, 16 * STACK_LOADS * (u.b + 1))
                    lhsT, rhs = stL[u.bp][:, u.h, rows], stR[u.bp][:, u.h, :]
                elif u.kind == "B":
                    if i == 0 and u.h == 0:
                        pe.wait_ge(s_lstack, 16 * LSTACK_LOADS * (u.b + 1))
                    lhsT, rhs = st1L[:, u.h, rows], st1R[:, u.h, :]
                else:
                    if i == 0:
                        pe.wait_ge(xaT_v[u.h].sem, xaT_v[u.h].upto(u.b, 1))
                    lhsT, rhs = xaT[:, rows], xT23[:, :]
                pe.matmul(S[i % 2][:, :], lhsT, rhs, start=True, stop=True).then_inc(s_score, 1)

            def transposes(u, half):
                pe.wait_ge(s_exp, 4 * u.g + 2 * half + 2)
                if due(n := 2 * (u.g - 1) + half + 1):
                    pe.wait_ge(s_hi, n)
                    pe.wait_ge(s_lo, n)
                for ii in range(2):
                    for j in range(NT):
                        ins = pe.transpose(T[half][:, N * ii + P * j:N * ii + P * (j + 1)],
                                           Pr[u.par][:, 2 * half + ii, P * j:P * (j + 1)], identf[:, :])
                ins.then_inc(s_tr, 1)

            def values(u, half):
                pe.wait_ge(s_hi, 2 * u.g + half + 1)
                pe.wait_ge(s_lo, 2 * u.g + half + 1)
                if half == 0:
                    if due(n := u.g):
                        pe.wait_ge(s_oev, n)
                    if u.h == 0 and u.kind == "A":
                        pe.wait_ge(q_v.sem, q_v.upto(u.b, 7))
                    if u.h == 0 and u.kind == "B":
                        pe.wait_ge(vb_v.sem, vb_v.upto(u.b, 5))
                for ii in range(2):
                    i = 2 * half + ii
                    for j in range(NT):
                        blk = slice(N * ii + P * j, N * ii + P * (j + 1))
                        if u.kind == "C":
                            ins = pe.matmul(O[:, D * i:D * (i + 1)], PTf[half][:, blk],
                                            (x2 if u.h == 0 else x3)[:, j, :], start=(j == 0), stop=(j == NT - 1))
                            continue
                        d, V = (D0, VA[u.bp]) if u.kind == "A" else (D1, VB)
                        dst = O[:, 4 * d * i:4 * d * (i + 1)].rearrange("p (k d) -> p k d", k=4)
                        for n, part in enumerate((PTh, PTl)):
                            ins = pe.matmul(dst, part[half][:, blk], V[:, j, :, d * u.h:d * (u.h + 1)],
                                            start=(j == 0 and n == 0), stop=(j == NT - 1 and n == 1))
                ins.then_inc(s_pv, 1)

            def turn(name, b, src):
                if due(n := x_index(name, b)):
                    pe.wait_ge(s_xfree, n)
                for t in range(NT):
                    ins = pe.transpose(X[:, P * t:P * (t + 1)], src[:, t, :], identf[:, :])
                ins.then_inc(s_x, 1)

            def turn_part(b, bp, k):
                pe.wait_ge(q_v.sem, q_v.upto(b, 2 * k + 3))
                if due(n := x_index("q" + "hml"[k], b)):
                    pe.wait_ge(s_xfree, n)
                for t in range(NT):
                    ins = pe.transpose(Xh[:, P * t:P * (t + 1)], VA[bp][:, t, k, :], identh[:, :])
                ins.then_inc(s_x, 1)

            def ff(b, c):
                pe.wait_ge(s_xfree, x_index(f"f{c}", b))
                pe.matmul(X[:, :], w1s[:, P * c:P * (c + 1)], yT[:, :], start=True, stop=True).then_inc(s_x, 1)

            def ff2(b):
                pe.wait_ge(s_xfree, x_index("w2", b))
                pe.wait_ge(gelu_v.sem, gelu_v.upto(b, 1))
                for t in range(NT):
                    for c in range(FC):
                        ins = pe.matmul(X[:, D * t:D * (t + 1)], hpre[:, c, P * t:P * (t + 1)], w2s[:, c, :],
                                        start=(c == 0), stop=(c == FC - 1))
                ins.then_inc(s_x, 1)

            def proj(b):
                pe.wait_ge(s_xfree, x_index("proj", b))
                for t in range(NT):
                    ins = pe.matmul(X[:, D * t:D * (t + 1)], x1T[:, P * t:P * (t + 1)], wlT[:, :], start=True, stop=True)
                ins.then_inc(s_x, 1)

            def logits(b):
                pe.wait_ge(s_xfree, x_index("lsd", b))
                pe.matmul(X[0:2 * H1, :], wa[:, :], x1T[:, :], start=True, stop=True).then_inc(s_x, 1)

            def half_slot(it, odd, at, now, back1, back2, back3):
                if present(it, 1):
                    b = it - 1
                    if at == 0:
                        pe.wait_ge(y_v.sem, y_v.upto(b, 2))
                        turn("yT", b, yn)
                    if at in (1, 1.5, 2, 2.5):
                        ff(b, int(2 * (at - 1)))
                if present(it, 2):
                    if at == 4:
                        pe.wait_ge(ln_x2.done.sem, ln_x2.done.upto(it - 2, NT))
                        turn("xT2", it - 2, x2)
                    if at == 8:
                        pe.wait_ge(ln_x3.done.sem, ln_x3.done.upto(it - 2, NT))
                        turn("xT3", it - 2, x3)
                if present(it, 1):
                    b = it - 1
                    if at == 4:
                        ff2(b)
                    if at == 6:
                        pe.wait_ge(lnf.done.sem, lnf.done.upto(b, NT))
                        turn("x1T", b, x1)
                    if at == 6.5:
                        proj(b)
                    if at == 7:
                        logits(b)
                if present(it, -1) and at in (10.5, 11, 11.5):
                    turn_part(it + 1, 1 - odd, int(2 * (at - 10.5)))
                if at == int(at):
                    if now:
                        scores(now, 0)
                        scores(now, 1)
                    if back1:
                        transposes(back1, 0)
                    if now:
                        scores(now, 2)
                    if back2:
                        values(back2, 0)
                else:
                    if back1:
                        transposes(back1, 1)
                    if now:
                        scores(now, 3)
                    if back2:
                        values(back2, 1)
            run_iterations(pe, half_slot)

            pe.wait_ge(s_flag, 2)
            pe.wait_ge(s_xfree, len(X_USES) * B)
            pe.matmul(X[0:1, 0:1], fmax[:, :], ones1[:, :], start=True, stop=True).then_inc(s_flag, 1)

            def general_pe(b):
                for k in range(2):
                    n = 2 * b + k
                    xk = x2 if k == 0 else x3
                    if k == 0:
                        pe.wait_ge(s_gload, 16 * 2 * (b + 1))
                    else:
                        pe.wait_ge(ln_g.done.sem, ln_g.done.upto(n - 1, NT))
                    for t in range(NT):
                        ins = pe.transpose(X[:, P * t:P * (t + 1)], xk[:, t, :], identf[:, :])
                    ins.then_inc(g_pe.sem, 1)
                    for i in range(NT):
                        pe.wait_ge(g_dve.sem, g_dve.upto(n, 4 + 12 * i))
                        for m in range(4):
                            ins = pe.matmul(T[m // 2][:, N * (m % 2):N * (m % 2 + 1)], Pr[1][:, m, P * i:P * (i + 1)],
                                            xT23[:, :], start=True, stop=True)
                        ins.then_inc(g_pe.sem, 1)
                    pe.wait_ge(g_act.sem, g_act.upto(n, 1 + NT))
                    for i in range(NT):
                        for j in range(NT):
                            ins = pe.transpose(T[i // 2][:, N * (i % 2) + P * j:N * (i % 2) + P * (j + 1)],
                                               Pr[0][:, i, P * j:P * (j + 1)], identf[:, :])
                    ins.then_inc(g_pe.sem, 1)
                    pe.wait_ge(g_act.sem, g_act.upto(n, 3 + NT))
                    for i in range(NT):
                        for j in range(NT):
                            ins = pe.matmul(O[:, D * i:D * (i + 1)], Y[1][:, i, P * j:P * (j + 1)], xk[:, j, :],
                                            start=(j == 0), stop=(j == NT - 1))
                    ins.then_inc(g_pe.sem, 1)
            general(pe, general_pe)


_INS = ["x", "adj", "L0_gnn_gamma1", "L0_gnn_beta1", "L0_gnn_gamma2", "L0_gnn_beta2", "L0_gnn_W1", "L0_gnn_b1",
        "L0_gnn_W2", "L0_gnn_b2", "L1_gnn_W", "L1_gnn_WT", "L1_gnn_b", "L1_gnn_a",
        "L2_gnn_a0", "L2_gnn_a1", "L2_gnn_a2", "L2_gnn_a3", "L3_gnn_a_0", "L3_gnn_a_1", "L3_gnn_a_2", "L3_gnn_a_3"]


def kernel(**inputs):
    import numpy as _np
    import concourse.bacc as _bacc
    from concourse import mybir as _mybir
    from concourse.bass_utils import run_bass_kernel_spmd as _run

    nc = _bacc.Bacc("TRN2", target_bir_lowering=False, num_devices=1)
    arrays, aps = {}, []
    for name in _INS:
        if name == "L1_gnn_WT":
            a = _np.ascontiguousarray(_np.asarray(inputs["L1_gnn_W"]).T)
        else:
            a = _np.ascontiguousarray(inputs[name])
        if name.startswith(("L2_", "L3_")):
            a = a.reshape(128, 1)
        arrays[f"in_{name}"] = a
        aps.append(nc.dram_tensor(f"in_{name}", a.shape, _mybir.dt.from_np(a.dtype), kind="ExternalInput").ap())
    out = nc.dram_tensor("out", (16, 512, 128), _mybir.dt.float32, kind="ExternalOutput").ap()
    adj_resnorm_kernel(nc, *aps[:14], aps[14:18], aps[18:22], out)
    r = _run(nc, [arrays], core_ids=[0])
    return r.results[0]["out"]
```

```python
from contextlib import ExitStack

import numpy as np
import concourse.bass as bass
from concourse import mybir

fp32 = mybir.dt.float32
bf16 = mybir.dt.bfloat16
fp16 = mybir.dt.float16
i32 = mybir.dt.int32
ALU = mybir.AluOpType
ACT = mybir.ActivationFunctionType
AX = mybir.AxisListType

B, N, D = 16, 512, 128
P = 128
NT = N // P
H0, H1 = 8, 4
D0, D1 = D // H0, D // H1
FF = 4 * D
FC = FF // P
W0 = 32
EPS = 1e-5
BIG = -9e15
TERMS_L = "hhhmml"
TERMS_R = "hmlhmh"
K0 = len(TERMS_L) * D0
STACK_LOADS = 2 * len(TERMS_L)
LSTACK_LOADS = 6
CONST_LOADS = 20 + 2 * H1
CONSTS = 12

ORDER = [("A", 0), ("A", 1), ("A", 2), ("A", 3), ("A", 4), ("A", 5), ("A", 6), ("A", 7), ("C", 0),
         ("B", 0), ("B", 1), ("B", 2), ("B", 3), ("C", 1)]
LAG = {"A": 0, "B": 1, "C": 2}
SLOTS = len(ORDER)
LOOP = (4, B - 2)
GROUP = P // 32
RESULTS = [("A", 0), ("A", 1), ("C", 0), ("B", 0), ("C", 1)]
X_USES = [("f0", 1), ("f1", 1), ("f2", 1), ("f3", 1), ("ob", 2), ("w2", 1), ("x1T", 1), ("proj", 1), ("lsd", 1),
          ("qh", -1), ("xT2", 2), ("oa0", 0), ("qm", -1), ("ql", -1), ("oa1", 0), ("xT3", 2), ("yT", 0)]
X_LAG = dict(X_USES)


def present(it, lag):
    return not isinstance(it, int) or 0 <= it - lag < B


def count_before(it, lags):
    if isinstance(it, int):
        return sum(min(max(it - lag, 0), B) for lag in lags)
    return len(lags) * it - sum(lags)


def index_in(it, lags, n):
    before = sum(1 for lag in lags[:n] if present(it, lag))
    return count_before(it, lags) + before


class Unit:
    def __init__(self, it, odd, pos):
        self.kind, self.h = ORDER[pos]
        lags = [LAG[k] for k, _ in ORDER]
        self.b = it - LAG[self.kind]
        self.bp = (odd + LAG[self.kind]) % 2
        self.g = index_in(it, lags, pos)
        self.par = self.g % 2 if isinstance(it, int) else (count_before(2, lags) + pos) % 2
        if self.kind != "A":
            leaky = [LAG[k] for k, _ in ORDER if k != "A"]
            self.leaky = index_in(it, leaky, sum(1 for k, _ in ORDER[:pos] if k != "A"))


def due(count):
    return not isinstance(count, int) or count > 0


def val(eng, count):
    return count if isinstance(count, int) else eng.compute_val(count)


class Steps:

    def __init__(self, sem, per):
        self.sem, self.per = sem, per

    def upto(self, b, k):
        return self.per * b + k


def adj_resnorm_kernel(nc, x, adj, gamma1, beta1, gamma2, beta2, W1, b1, W2, b2, Wl1, WTl1, bl1, al1,
                       a2s, a3s, out):
    ctx = ExitStack()
    with ctx:
        def sb(name, shape, dt=fp32):
            return ctx.enter_context(nc.sbuf_tensor(name, shape, dt))

        def sem(name):
            return ctx.enter_context(nc.semaphore(name))

        def steps(name, per):
            return Steps(sem(name), per)

        identf, identh = sb("identf", [P, P]), sb("identh", [P, P], bf16)
        g1b, be1b, g2b, be2b, b2b, bl1b = (sb(n, [P, D]) for n in ("g1b", "be1b", "g2b", "be2b", "b2b", "bl1b"))
        w1s, w2s, b1c = sb("w1s", [P, FF]), sb("w2s", [P, FC, D]), sb("b1c", [P, FC])
        wl, wlT, blc = sb("wl", [P, D]), sb("wlT", [P, D]), sb("blc", [P, 1])
        head_a = sb("head_a", [P, 2 * H1])
        wa, wab = sb("wa", [P, 2 * H1]), sb("wab", [2 * H1, 1])
        ac = [sb("a2c", [P, 4]), sb("a3c", [P, 4])]
        mhalf = sb("mhalf", [P, NT])
        Y = [sb(f"Y{i}", [P, NT, N]) for i in range(2)]
        Pr = [sb(f"Pr{i}", [P, NT, N]) for i in range(2)]
        PT = [sb(f"PT{i}", [P, NT, N]) for i in range(2)]
        mx = [sb(f"mx{i}", [P, NT]) for i in range(2)]
        negmx = [sb(f"negmx{i}", [P, NT]) for i in range(2)]
        nm = [sb(f"nm{i}", [P, NT]) for i in range(2)]
        xin = [sb(f"xin{i}", [P, NT, D]) for i in range(2)]
        adji = [sb(f"adji{i}", [P, NT, N], i32) for i in range(2)]
        bias0 = [sb(f"bias0{i}", [P, NT, N], bf16) for i in range(2)]
        bias1 = [sb(f"bias1{i}", [P, NT, N], bf16) for i in range(2)]
        stL = [sb(f"stL{i}", [K0, H0, N], bf16) for i in range(2)]
        stR = [sb(f"stR{i}", [K0, H0, N], bf16) for i in range(2)]
        qT = {s: sb(f"qT{s}", [P, N], bf16) for s in "hml"}
        QP = sb("QP", [P, NT, 3, D], bf16)
        VA = [sb(f"VA{i}", [P, NT, H0, W0]) for i in range(2)]
        VB = sb("VB", [P, NT, D])
        OT = [sb(f"OT{i}", [P, N]) for i in range(3)]
        OC = sb("OC", [P, NT, D])
        qn = sb("qn", [P, NT, D])
        rdA = sb("rdA", [P, NT, H0])
        xr, yn, yT = sb("xr", [P, NT, D]), sb("yn", [P, NT, D]), sb("yT", [P, N])
        hpre = sb("hpre", [P, FC, N])
        sumx, x1, x1T = sb("sumx", [P, NT, D]), sb("x1", [P, NT, D]), sb("x1T", [P, N])
        lsd = sb("lsd", [2 * H1, N])
        lpart = {s: sb(f"lp{s}", [2 * H1, N], bf16) for s in "hml"}
        st1L, st1R = sb("st1L", [K0, H1, N], bf16), sb("st1R", [K0, H1, N], bf16)
        cB, rdB, x2 = sb("cB", [P, NT, D]), sb("rdB", [P, H1, NT]), sb("x2", [P, NT, D])
        xT23, xaT = sb("xT23", [P, N]), sb("xaT", [P, N])
        sumB = sb("sumB", [P, H1, NT])
        sums, rdC = sb("sums", [P, 2, NT]), sb("rdC", [P, 2, NT])
        x3, xo = sb("x3", [P, NT, D]), sb("xo", [P, NT, D])

        def pb(name, n):
            return ctx.enter_context(nc.psum_tensor(name, [P, n * N], fp32))

        S = [pb("S0", 1), pb("S1", 1)]
        T = [pb("T0", 2), pb("T1", 2)]
        O, X = pb("O", 1), pb("X", 1)
        Xh = X[:, :].bitcast(bf16)[:, 0:N]

        junk, flags = sb("junk", [P, NT, N], bf16), sb("flags", [P, B])
        fmax, ones1, minus1, flag = sb("fmax", [P, 1]), sb("ones1", [P, 1]), sb("minus1", [P, 1]), sb("flag", [1, 1], i32)
        saved = nc.dram_tensor("layer1_result", (B, N, D), fp32, kind="Internal").ap()

        parts_dram = nc.dram_tensor("query_parts", (2, 3, P, N), bf16, kind="Internal").ap()

        s_score = sem("s_score")
        s_read = sem("s_read")
        s_neg = sem("s_neg")
        s_leak = sem("s_leak")
        s_exp = sem("s_exp")
        s_tr = sem("s_tr")
        s_copied = sem("s_copied")
        s_pv = sem("s_pv")
        s_oev = sem("s_oev")
        s_x = sem("s_x")
        s_xfree = sem("s_xfree")
        s_adj, s_xin = sem("s_adj"), sem("s_xin")
        s_cload, s_part, s_stack, s_lstack, s_out = sem("s_cload"), sem("s_part"), sem("s_stack"), sem("s_lstack"), sem("s_out")
        s_saved = sem("s_saved")
        s_looked = sem("s_looked")
        s_flag = sem("s_flag")
        s_const = sem("s_const")
        s_cv = sem("s_cv")
        s_cp = sem("s_cp")
        b0_done, b1_done = steps("b0_done", 1), steps("b1_done", 1)
        q_v = steps("q_v", 7)
        cA_v, cA_r = steps("cA_v", 1), steps("cA_r", 4)
        y_v = steps("y_v", 2)
        gelu_v = steps("gelu_v", 1)
        sum_v = steps("sum_v", 2)
        lp_v = steps("lp_v", 5)
        cB_v, cB_r = steps("cB_v", 1), steps("cB_r", 2)
        xaT_v = [steps("xaT2_v", 1), steps("xaT3_v", 1)]
        oc_r = [steps("oc2_r", 1), steps("oc3_r", 1)]
        oc_v = [steps("oc2_v", NT), steps("oc3_v", NT)]

        g_pe, g_act, g_dve = steps("g_pe", 3 + NT), steps("g_act", 4 + NT), steps("g_dve", 4 + 12 * NT + 1 + NT)
        s_gload = sem("s_gload")

        class Norm:

            def __init__(self, name):
                self.st, self.mv = sb(name + "_st", [P, NT, 6]), sb(name + "_mv", [P, NT, 2])
                self.ve, self.rs = sb(name + "_ve", [P, NT]), sb(name + "_rs", [P, NT])
                self.stat = steps(name + "_stat", 2 * NT)
                self.root = steps(name + "_root", 2)
                self.done = steps(name + "_done", NT)

            def stats(self, dve, b, src):
                if due(n := self.root.upto(b, 0)):
                    dve.wait_ge(self.root.sem, n)
                for t in range(NT):
                    dve.bn_stats(self.st[:, t, :], src[:, t, :]).then_inc(self.stat.sem, 1)
                for t in range(NT):
                    n = val(dve, self.stat.upto(b, t + 1))
                    dve.wait_ge(s_const, 1)
                    dve.wait_ge(self.stat.sem, n)
                    dve.bn_aggr(self.mv[:, t, :], self.st[:, t, :]).then_inc(self.stat.sem, 1)

            def roots(self, pool, b):
                ready, free = val(pool, self.stat.upto(b, 2 * NT)), val(pool, self.done.upto(b, 0))
                pool.wait_ge(s_const, 1)
                pool.wait_ge(self.stat.sem, ready)
                if due(free):
                    pool.wait_ge(self.done.sem, free)
                pool.tensor_scalar(self.ve[:, :], self.mv[:, :, 1], EPS, None, ALU.add).then_inc(self.root.sem, 1)
                pool.wait_ge(self.root.sem, self.root.upto(b, 1))
                pool.tensor_tensor(self.rs[:, :], self.ve[:, :], mhalf[:, :], ALU.pow).then_inc(self.root.sem, 1)

            def scale(self, dve, b, src, dst):
                dve.wait_ge(self.root.sem, self.root.upto(b, 2))
                for t in range(NT):
                    dve.tensor_scalar(dst[:, t, :], src[:, t, :], self.mv[:, t, 0:1], self.rs[:, t:t + 1],
                                      ALU.subtract, ALU.mult).then_inc(self.done.sem, 1)

        ln1, ln2, lnf, ln_x2, ln_x3, ln_out, ln_g = (
            Norm(name) for name in ("ln1", "ln2", "lnf", "ln_x2", "ln_x3", "ln_out", "ln_g"))

        ctx.enter_context(nc.allow_non_contiguous_dma(reason="columns of a few hundred constants, once"))
        block = ctx.enter_context(nc.Block())

        def general(eng, program, end=None):
            eng.wait_ge(s_flag, 4)
            raised = eng.value_load(flag[0:1, 0:1], min_val=0, max_val=1)
            with eng.If(raised > 0):
                with eng.Fori(0, B) as b:
                    program(b)
                if end:
                    end()

        LAGS = [LAG[k] for k, _ in ORDER]
        POS = {u: p for p, u in enumerate(ORDER)}

        def g_of(kind, h, b):
            return index_in(b + LAG[kind], LAGS, POS[(kind, h)])

        def after(kind, h, b):
            return g_of(kind, h, b) + 1 if not isinstance(b, int) or b >= 0 else 0

        def x_index(name, b):
            names, lags = zip(*X_USES)
            return index_in(b + X_LAG[name], lags, names.index(name))

        def result_index(kind, group, b):
            return index_in(b + LAG[kind], [LAG[k] for k, _ in RESULTS], RESULTS.index((kind, group)))

        def previous(count, b):
            return count if not isinstance(b, int) or b >= 1 else 0

        def run_iterations(eng, half_slot):
            def iteration(it, odd, units):
                for p in range(SLOTS):
                    unit = Unit(it, odd, p) if present(it, LAG[ORDER[p][0]]) else None
                    units = [unit] + units[:3]
                    half_slot(it, odd, p, *units)
                    half_slot(it, odd, p + 0.5, *units)
                return units

            def last_units(it, odd):
                return [Unit(it, odd, SLOTS - 1 - k) for k in range(3)]

            units = [None] * 3
            for it in range(-1, LOOP[0]):
                units = iteration(it, it % 2, units)
            with eng.Fori(*LOOP, 2) as it:
                middle = iteration(it, LOOP[0] % 2, last_units(it - 1, (LOOP[0] - 1) % 2))
                iteration(it + 1, (LOOP[0] + 1) % 2, middle)
            units = last_units(LOOP[1] - 1, (LOOP[1] - 1) % 2)
            for it in range(LOOP[1], B + 3):
                units = iteration(it, it % 2, units)

        def tiles(dram, b):
            return dram[bass.ds(b, 1), :, :].rearrange("a (t p) n -> p (a t) n", p=P)

        @block.sync
        def _(sp):
            def load(dst, src):
                sp.dma_start(dst, src).then_inc(s_cload, 16)

            def row(v):
                return v.rearrange("(a n) -> a n", a=1).broadcast_to([P, D])
            for dst, v in ((g1b, gamma1), (be1b, beta1), (g2b, gamma2), (be2b, beta2), (b2b, b2), (bl1b, bl1)):
                load(dst[:, :], row(v))
            load(w1s[:, :], W1)
            load(w2s[:, :, :], W2.rearrange("(c p) n -> p c n", p=P))
            load(b1c[:, :], b1.rearrange("(c p) -> p c", p=P))
            load(wl[:, :], Wl1)
            load(wlT[:, :], WTl1)
            load(blc[:, :], bl1.rearrange("(p a) -> p a", a=1))
            for c, vs in ((ac[0], a2s), (ac[1], a3s)):
                for k in range(4):
                    load(c[:, k:k + 1], vs[k])
            sp.wait_ge(s_const, 2)
            for h in range(H1):
                for k in range(2):
                    load(head_a[D1 * h:D1 * (h + 1), H1 * k + h:H1 * k + h + 1],
                         al1[h:h + 1, D1 * k:D1 * (k + 1)].rearrange("a p -> p a"))

            def load_adj(b, bp):
                used, looked = val(sp, b1_done.upto(b - 1, 0)), val(sp, b - 1)
                if due(used):
                    sp.wait_ge(b1_done.sem, used)
                if due(looked):
                    sp.wait_ge(s_looked, looked)
                sp.dma_start(adji[bp][:, :, :], tiles(adj, b)).then_inc(s_adj, 16)

            def load_x(b, bp):
                if due(n := sum_v.upto(b - 1, 0)):
                    sp.wait_ge(sum_v.sem, n)
                sp.dma_start(xin[bp][:, :, :], tiles(x, b)).then_inc(s_xin, 16)

            def keep_part(k, b, bp):
                evacuated, read_back = val(sp, x_index("q" + "hml"[k], b) + 1), val(sp, 16 * STACK_LOADS * (b - 1))
                sp.wait_ge(s_xfree, evacuated)
                if due(read_back):
                    sp.wait_ge(s_stack, read_back)
                sp.dma_start(parts_dram[bp, k, :, :], qT["hml"[k]][:, :]).then_inc(s_part, 16)

            def stack(b, bp):
                kept, scored = val(sp, 16 * 3 * (b + 1)), val(sp, 4 * after("A", H0 - 1, b - 2))
                sp.wait_ge(s_part, kept)
                if due(scored):
                    sp.wait_ge(s_score, scored)
                part = parts_dram[bp].rearrange("s (h d) n -> s d h n", d=D0)
                for st, terms in ((stL, TERMS_L), (stR, TERMS_R)):
                    for k, s in enumerate(terms):
                        sp.dma_start(st[bp][D0 * k:D0 * (k + 1), :, :], part["hml".index(s)]).then_inc(s_stack, 16)

            def lstack(b, bp):
                split, scored = val(sp, lp_v.upto(b, 5)), val(sp, previous(4 * after("B", H1 - 1, b - 1), b))
                sp.wait_ge(lp_v.sem, split)
                if due(scored):
                    sp.wait_ge(s_score, scored)
                for k, s in enumerate("hml"):
                    sp.dma_start(st1L[k:k + 1, :, :], lpart[s][0:H1, :]).then_inc(s_lstack, 16)
                    sp.dma_start(st1R[3 + k:4 + k, :, :], lpart[s][H1:2 * H1, :]).then_inc(s_lstack, 16)

            def save(b, bp):
                sp.wait_ge(ln_x2.done.sem, ln_x2.done.upto(b, NT))
                sp.dma_start(tiles(saved, b), x2[:, :, :]).then_inc(s_saved, 16)

            def store(b, bp):
                sp.wait_ge(ln_out.done.sem, ln_out.done.upto(b, NT))
                sp.dma_start(tiles(out, b), xo[:, :, :]).then_inc(s_out, 16)

            def half_slot(it, odd, at, *units):
                if present(it, -1):
                    ahead = it + 1, 1 - odd
                    if at == 0.5:
                        load_x(*ahead)
                    if at == 1.5:
                        load_adj(*ahead)
                    if at in (6.5, 8.5, 9):
                        keep_part((6.5, 8.5, 9).index(at), *ahead)
                    if at == 9.5:
                        stack(*ahead)
                if present(it, 1) and at == 7.5:
                    lstack(it - 1, 1 - odd)
                if present(it, 2) and at == 4:
                    save(it - 2, odd)
                if present(it, 3) and at == 4:
                    store(it - 3, 1 - odd)
            run_iterations(sp, half_slot)
            sp.wait_ge(s_out, 16 * B)
            sp.wait_ge(s_saved, 16 * B)

            def general_sp(b):
                sp.wait_ge(s_out, val(sp, 16 * (b + B)))
                sp.dma_start(x2[:, :, :], tiles(saved, b)).then_inc(s_gload, 16)
                sp.dma_start(adji[0][:, :, :], tiles(adj, b)).then_inc(s_gload, 16)
                sp.wait_ge(ln_g.done.sem, NT * (2 * b + 2))
                sp.dma_start(tiles(out, b), xo[:, :, :]).then_inc(s_out, 16)
            general(sp, general_sp, lambda: sp.wait_ge(s_out, 16 * 2 * B))

        @block.gpsimd
        def _(pool):
            pool.memset(identf[:, :], 0.0).then_inc(s_const, 1)
            pool.memset(head_a[:, :], 0.0).then_inc(s_const, 1)
            pool.memset(identh[:, :], 0.0).then_inc(s_const, 1)
            pool.wait_ge(s_const, 3)
            for m in (identf, identh):
                pool.affine_select(out=m[:, :], in_=m[:, :], compare_op=ALU.not_equal, fill=1.0, base=0,
                                   pattern=[[-1, P]], channel_multiplier=1).then_inc(s_const, 1)
            pool.memset(mhalf[:, :], -0.5).then_inc(s_const, 1)
            for st in (st1L, st1R):
                pool.memset(st[:, :, :], 0.0).then_inc(s_const, 1)
            pool.wait_ge(s_const, 8)
            for st in (st1L, st1R):
                pool.memset(st[0:6, :, :], 1.0).then_inc(s_const, 1)
            for v in VA:
                pool.memset(v[:, :, :, D0:W0], 1.0).then_inc(s_const, 1)
            pool.wait_ge(s_const, CONSTS)
            pool.wait_ge(s_cload, 16 * CONST_LOADS)

            def make_bias0(b, bp):
                arrived, used = val(pool, 16 * (b + 1)), val(pool, 4 * after("A", H0 - 1, b - 2))
                pool.wait_ge(s_const, 1)
                pool.wait_ge(s_adj, arrived)
                if due(used):
                    pool.wait_ge(s_read, used)
                pool.tensor_scalar(bias0[bp][:, :, :], adji[bp][:, :, :], 0.0, BIG, ALU.is_le,
                                   ALU.mult).then_inc(b0_done.sem, 1)

            def round_off(v, b, k, part, left, src):
                n = val(pool, v.upto(b, k - 1))
                pool.wait_ge(s_const, 1)
                pool.wait_ge(v.sem, n)
                pool.tensor_copy(part, src).then_inc(v.sem, 1)
                pool.wait_ge(v.sem, v.upto(b, k))
                pool.tensor_tensor(left, src, part, ALU.subtract).then_inc(v.sem, 1)

            def bc(t):
                return t[:, :].rearrange("p (a d) -> p a d", a=1).broadcast_to([P, NT, D])

            def q_affine(b, bp):
                pool.wait_ge(ln1.done.sem, ln1.done.upto(b, NT))
                pool.tensor_tensor(qn[:, :, :], qn[:, :, :], bc(g1b), ALU.mult).then_inc(q_v.sem, 1)
                product, used = val(pool, q_v.upto(b, 1)), val(pool, after("A", H0 - 1, b - 2))
                pool.wait_ge(q_v.sem, product)
                if due(used):
                    pool.wait_ge(s_pv, used)
                heads = lambda m: m.rearrange("p t (h d) -> p t h d", h=H0)
                pool.tensor_tensor(VA[bp][:, :, :, 0:D0], heads(qn[:, :, :]), heads(bc(be1b)), ALU.add).then_inc(q_v.sem, 1)

            def q_part(b, bp, k):
                heads = lambda m: m.rearrange("p t (h d) -> p t h d", h=H0)
                part = QP[:, :, k, :]
                if k == 0:
                    read = val(pool, previous(x_index("ql", b - 1) + 1, b))
                    if due(read):
                        pool.wait_ge(s_x, read)
                    round_off(q_v, b, 3, heads(part), heads(qn[:, :, :]), VA[bp][:, :, :, 0:D0])
                if k == 1:
                    round_off(q_v, b, 5, part, qn[:, :, :], qn[:, :, :])
                if k == 2:
                    n = val(pool, q_v.upto(b, 6))
                    pool.wait_ge(s_const, 1)
                    pool.wait_ge(q_v.sem, n)
                    pool.tensor_copy(part, qn[:, :, :]).then_inc(q_v.sem, 1)

            def combine_a(b, bp):
                pool.wait_ge(cA_r.sem, cA_r.upto(b, 4))
                pool.tensor_tensor(xr[:, :, :], xr[:, :, :], xin[bp][:, :, :], ALU.add).then_inc(cA_v.sem, 1)

            def combine_b(b):
                pool.wait_ge(cB_r.sem, cB_r.upto(b, 2))
                pool.tensor_tensor(cB[:, :, :], cB[:, :, :], x1[:, :, :], ALU.add).then_inc(cB_v.sem, 1)

            def y_affine(b, bp):
                pool.wait_ge(ln2.done.sem, ln2.done.upto(b, NT))
                pool.tensor_tensor(yn[:, :, :], yn[:, :, :], bc(g2b), ALU.mult).then_inc(y_v.sem, 1)
                pool.wait_ge(y_v.sem, y_v.upto(b, 1))
                pool.tensor_tensor(yn[:, :, :], yn[:, :, :], bc(be2b), ALU.add).then_inc(y_v.sem, 1)

            def add_up(b, bp):
                if due(n := lnf.done.upto(b, 0)):
                    pool.wait_ge(lnf.done.sem, n)
                pool.tensor_tensor(sumx[:, :, :], xr[:, :, :], bc(b2b), ALU.add).then_inc(sum_v.sem, 1)
                pool.wait_ge(sum_v.sem, sum_v.upto(b, 1))
                pool.tensor_tensor(sumx[:, :, :], sumx[:, :, :], xin[bp][:, :, :], ALU.add).then_inc(sum_v.sem, 1)

            def l_parts(b):
                rows, free = val(pool, x_index("lsd", b) + 1), val(pool, 16 * LSTACK_LOADS * b)
                pool.wait_ge(s_const, 1)
                pool.wait_ge(s_xfree, rows)
                if due(free):
                    pool.wait_ge(s_lstack, free)
                pool.tensor_copy(lpart["h"][:, :], lsd[:, :]).then_inc(lp_v.sem, 1)
                pool.wait_ge(lp_v.sem, lp_v.upto(b, 1))
                pool.tensor_tensor(lsd[:, :], lsd[:, :], lpart["h"][:, :], ALU.subtract).then_inc(lp_v.sem, 1)
                round_off(lp_v, b, 3, lpart["m"][:, :], lsd[:, :], lsd[:, :])
                n = val(pool, lp_v.upto(b, 4))
                pool.wait_ge(s_const, 1)
                pool.wait_ge(lp_v.sem, n)
                pool.tensor_copy(lpart["l"][:, :], lsd[:, :]).then_inc(lp_v.sem, 1)

            def half_slot(it, odd, at, *units):
                if present(it, 1) and at == 0:
                    add_up(it - 1, 1 - odd)
                if present(it, 2):
                    if at == 2:
                        combine_b(it - 2)
                    if at == 2.5:
                        ln_x2.roots(pool, it - 2)
                if present(it, 3) and at == 2.5:
                    ln_out.roots(pool, it - 3)
                if present(it, 1):
                    if at == 3.5:
                        lnf.roots(pool, it - 1)
                    if at == 5.5:
                        l_parts(it - 1)
                if present(it, -1):
                    if at == 3:
                        ln1.roots(pool, it + 1)
                    if at == 4:
                        q_affine(it + 1, 1 - odd)
                    if at in (4.5, 7, 7.5):
                        q_part(it + 1, 1 - odd, (4.5, 7, 7.5).index(at))
                    if at == 8:
                        make_bias0(it + 1, 1 - odd)
                if present(it, 0) and at == 11:
                    combine_a(it, odd)
                if present(it, 2) and at == 11.5:
                    ln_x3.roots(pool, it - 2)
                if present(it, 0):
                    if at == 12:
                        ln2.roots(pool, it)
                    if at == 12.5:
                        y_affine(it, odd)
            run_iterations(pool, half_slot)

            def general_pool(b):
                for k in range(2):
                    n = 2 * b + k
                    ready = val(pool, ln_g.stat.upto(n, 2 * NT))
                    pool.wait_ge(s_const, 1)
                    pool.wait_ge(ln_g.stat.sem, ready)
                    pool.tensor_scalar(ln_g.ve[:, :], ln_g.mv[:, :, 1], EPS, None, ALU.add).then_inc(ln_g.root.sem, 1)
                    pool.wait_ge(ln_g.root.sem, ln_g.root.upto(n, 1))
                    pool.tensor_tensor(ln_g.rs[:, :], ln_g.ve[:, :], mhalf[:, :], ALU.pow).then_inc(ln_g.root.sem, 1)
            general(pool, general_pool)

        @block.scalar
        def _(act):
            act.wait_ge(s_cv, 4)

            def exps(u):
                if u.kind == "A":
                    act.wait_ge(s_neg, u.g + 1)
                else:
                    act.wait_ge(s_leak, u.leaky + 1)
                if due(n := 2 * (u.g - 1)):
                    act.wait_ge(s_tr, n)
                if u.kind == "C" and due(n := oc_r[u.h].upto(u.b, 0)):
                    act.wait_ge(oc_r[u.h].sem, n)
                if u.kind == "B" and due(n := cB_r.upto(u.b, 0)):
                    act.wait_ge(cB_r.sem, n)
                for i in range(NT):
                    more = {} if u.kind == "A" else {"accum_out": (sums if u.kind == "C" else sumB)[:, u.h, i:i + 1]}
                    act.activation(Pr[u.par][:, i, :], Y[u.par][:, i, :], ACT.Exp, bias=nm[u.par][:, i:i + 1],
                                   scale=D0 ** -0.5 if u.kind == "A" else 1.0, **more).then_inc(s_exp, 1)

            def copy(u, half):
                act.wait_ge(s_tr, 2 * u.g + half + 1)
                if due(n := u.g - 1):
                    act.wait_ge(s_pv, n)
                act.activation(PT[u.par][:, 2 * half:2 * half + 2, :], T[half][:, :].rearrange("p (i n) -> p i n", i=2),
                               ACT.Copy).then_inc(s_copied, 1)

            def result(u):
                if u.kind == "C":
                    norm = ln_x3 if u.h else ln_out
                    if due(n := norm.done.upto(u.b + u.h, 0)):
                        act.wait_ge(norm.done.sem, n)
                    act.wait_ge(s_pv, u.g + 1)
                    act.activation(OC[:, :, :], O[:, :].rearrange("p (t c) -> p t c", t=NT), ACT.Copy).then_inc(s_oev, 1)
                elif u.h % GROUP == GROUP - 1:
                    name = f"oa{u.h // GROUP}" if u.kind == "A" else "ob"
                    if due(n := previous(x_index(name, u.b - 1) + 1, u.b)):
                        act.wait_ge(s_x, n)
                    act.wait_ge(s_pv, u.g + 1)
                    ot = OT[u.h // GROUP if u.kind == "A" else 2]
                    act.activation(ot[:, :], O[:, :], ACT.Copy).then_inc(s_oev, 1)

            def evacuate(name, b, dst, src):
                act.wait_ge(s_x, x_index(name, b) + 1)
                act.activation(dst, src, ACT.Copy).then_inc(s_xfree, 1)

            def gelu(b):
                act.wait_ge(s_xfree, x_index("f3", b) + 1)
                act.activation(hpre[:, :, :], hpre[:, :, :], ACT.Gelu).then_inc(gelu_v.sem, 1)

            def look(b, bp):
                act.wait_ge(s_adj, 16 * (b + 1))
                act.activation(junk[:, :, :], adji[bp][:, :, :], ACT.Relu, bias=minus1[:, 0:1],
                               accum_out=flags[:, bass.ds(b, 1)]).then_inc(s_looked, 1)

            def half_slot(it, odd, at, now, back1, back2, back3):
                if present(it, 1):
                    if at == 2:
                        gelu(it - 1)
                    if at == 4.5:
                        evacuate("x1T", it - 1, x1T[:, :], X[:, :])
                if present(it, -1) and at in (6, 8, 8.5):
                    k = (6, 8, 8.5).index(at)
                    if due(n := 16 * (3 * it + 3)):
                        act.wait_ge(s_part, n)
                    evacuate("q" + "hml"[k], it + 1, qT["hml"[k]][:, :], Xh)
                if present(it, 2):
                    if at == 6.5:
                        evacuate("xT2", it - 2, xT23[:, :], X[:, :])
                    if at == 12.5:
                        evacuate("xT3", it - 2, xT23[:, :], X[:, :])
                if present(it, -1) and at == 7:
                    look(it + 1, 1 - odd)
                if present(it, 0) and at == 13.5:
                    evacuate("yT", it, yT[:, :], X[:, :])
                if at == int(at):
                    if back1:
                        exps(back1)
                    if back3:
                        result(back3)
                elif back2:
                    copy(back2, 0)
                    copy(back2, 1)
            run_iterations(act, half_slot)

            def general_act(b):
                for k in range(2):
                    n = 2 * b + k
                    act.wait_ge(g_pe.sem, g_pe.upto(n, 1))
                    act.activation(xT23[:, :], X[:, :], ACT.Copy).then_inc(g_act.sem, 1)
                    act.wait_ge(g_dve.sem, g_dve.upto(n, 4 + 12 * NT))
                    for i in range(NT):
                        act.activation(Pr[0][:, i, :], Y[0][:, i, :], ACT.Exp, bias=nm[0][:, i:i + 1],
                                       accum_out=sums[:, 0, i:i + 1]).then_inc(g_act.sem, 1)
                    act.wait_ge(g_pe.sem, g_pe.upto(n, 2 + NT))
                    for half in range(2):
                        act.activation(Y[1][:, 2 * half:2 * half + 2, :], T[half][:, :].rearrange("p (i n) -> p i n", i=2),
                                       ACT.Copy).then_inc(g_act.sem, 1)
                    act.wait_ge(g_pe.sem, g_pe.upto(n, 3 + NT))
                    act.activation(OC[:, :, :], O[:, :].rearrange("p (t c) -> p t c", t=NT), ACT.Copy).then_inc(g_act.sem, 1)
            general(act, general_act)

        @block.vector
        def _(dve):
            dve.wait_ge(s_cp, 2)
            dve.tensor_copy(wa[:, :], O[:, 0:2 * H1]).then_inc(s_cv, 1)
            dve.tensor_copy(wab[:, :], X[0:2 * H1, 0:1]).then_inc(s_cv, 1)
            dve.wait_ge(s_const, CONSTS)
            dve.wait_ge(s_cload, 16 * CONST_LOADS)
            dve.sem_inc(s_cv, 1)
            dve.memset(minus1[:, :], -1.0).then_inc(s_cv, 1)
            dve.memset(ones1[:, :], 1.0).then_inc(s_flag, 1)

            def mask(u, i):
                scored, left = val(dve, 4 * u.g + i + 1), val(dve, 4 * (u.g - 1))
                bias, made = (bias0, b0_done) if u.kind == "A" else (bias1, b1_done)
                biased = val(dve, made.upto(u.b, 1))
                dve.wait_ge(s_const, 1)
                dve.wait_ge(s_score, scored)
                if i == 0:
                    if due(left):
                        dve.wait_ge(s_exp, left)
                    dve.wait_ge(made.sem, biased)
                dve.tensor_tensor_reduce(out=Y[u.par][:, i, :], in0=S[i % 2][:, :], in1=bias[u.bp][:, i, :], scale=1.0,
                                         scalar=-3e38, op0=ALU.add, op1=ALU.max,
                                         accum_out=mx[u.par][:, i:i + 1]).then_inc(s_read, 1)

            def maxima(u):
                p = u.par
                dve.wait_ge(s_read, 4 * u.g + 4)
                if u.kind == "A":
                    dve.tensor_scalar(nm[p][:, :], mx[p][:, :], -D0 ** -0.5, None, ALU.mult).then_inc(s_neg, 1)
                    return
                dve.tensor_scalar(negmx[p][:, :], mx[p][:, :], -1.0, None, ALU.mult).then_inc(s_neg, 1)
                dve.scalar_tensor_tensor(out=Y[p][:, :, :], in0=Y[p][:, :, :], scalar=0.2, in1=Y[p][:, :, :],
                                         op0=ALU.mult, op1=ALU.max)
                dve.wait_ge(s_neg, u.g + 1)
                dve.scalar_tensor_tensor(out=nm[p][:, :], in0=mx[p][:, :], scalar=-0.2, in1=negmx[p][:, :],
                                         op0=ALU.mult, op1=ALU.min).then_inc(s_leak, 1)

            def make_bias1(b, bp):
                dve.wait_ge(s_adj, 16 * (b + 1))
                dve.wait_ge(b0_done.sem, b0_done.upto(b, 1))
                dve.tensor_scalar(bias1[bp][:, :, :], adji[bp][:, :, :], 1.0, BIG, ALU.not_equal,
                                  ALU.mult).then_inc(b1_done.sem, 1)

            def group_a(b, k):
                heads = X[:, :].rearrange("p (t h d) -> p t h d", t=NT, h=GROUP)
                mine = slice(GROUP * k, GROUP * (k + 1))
                if k == 0 and due(n := sum_v.upto(b, 0)):
                    dve.wait_ge(sum_v.sem, n)
                dve.wait_ge(s_x, x_index(f"oa{k}", b) + 1)
                dve.reciprocal(rdA[:, :, mine], heads[:, :, :, D0]).then_inc(cA_r.sem, 1)
                dve.wait_ge(cA_r.sem, cA_r.upto(b, 2 * k + 1))
                over = rdA[:, :, mine].rearrange("p t (h a) -> p t h a", a=1).broadcast_to([P, NT, GROUP, D0])
                dst = xr[:, :, D0 * GROUP * k:D0 * GROUP * (k + 1)].rearrange("p t (h d) -> p t h d", h=GROUP)
                dve.tensor_tensor(dst, heads[:, :, :, 0:D0], over, ALU.mult).then_inc(cA_r.sem, 1)
                dve.wait_ge(cA_r.sem, cA_r.upto(b, 2 * k + 2))
                dve.sem_inc(s_xfree, 1)

            def group_b(b):
                dve.wait_ge(s_x, x_index("ob", b) + 1)
                dve.reciprocal(rdB[:, :, :], sumB[:, :, :]).then_inc(cB_r.sem, 1)
                if due(n := ln_x2.done.upto(b, 0)):
                    dve.wait_ge(ln_x2.done.sem, n)
                dve.wait_ge(cB_r.sem, cB_r.upto(b, 1))
                over = rdB[:, :, :].rearrange("p h (t a) -> p h t a", a=1).broadcast_to([P, H1, NT, D1])
                dst = cB[:, :, :].rearrange("p t (h d) -> p h t d", h=H1)
                src = X[:, :].rearrange("p (t h d) -> p h t d", t=NT, h=H1)
                dve.tensor_tensor(dst, src, over, ALU.mult).then_inc(cB_r.sem, 1)
                dve.wait_ge(cB_r.sem, cB_r.upto(b, 2))
                dve.sem_inc(s_xfree, 1)

            def ff_bias(b, c):
                dve.wait_ge(s_x, x_index(f"f{c}", b) + 1)
                dve.tensor_scalar(hpre[:, c, :], X[:, :], b1c[:, c:c + 1], None, ALU.add).then_inc(s_xfree, 1)

            def mlp_residual(b):
                dve.wait_ge(sum_v.sem, sum_v.upto(b, 2))
                dve.wait_ge(s_x, x_index("w2", b) + 1)
                dve.tensor_tensor(sumx[:, :, :], X[:, :].rearrange("p (t d) -> p t d", t=NT), sumx[:, :, :],
                                  ALU.add).then_inc(s_xfree, 1)

            def projected(b):
                if due(n := previous(after("B", H1 - 1, b - 1), b)):
                    dve.wait_ge(s_pv, n)
                dve.wait_ge(s_x, x_index("proj", b) + 1)
                bias = bl1b[:, :].rearrange("p (a d) -> p a d", a=1).broadcast_to([P, NT, D])
                dve.tensor_tensor(VB[:, :, :], X[:, :].rearrange("p (t d) -> p t d", t=NT), bias,
                                  ALU.add).then_inc(s_xfree, 1)

            def logits(b):
                if due(n := lp_v.upto(b, 0)):
                    dve.wait_ge(lp_v.sem, n)
                dve.wait_ge(s_x, x_index("lsd", b) + 1)
                dve.tensor_scalar(lsd[:, :], X[0:2 * H1, :], wab[:, 0:1], None, ALU.add).then_inc(s_xfree, 1)

            def scaled(k, b):
                dve.wait_ge(s_xfree, x_index(f"xT{k + 2}", b) + 1)
                dve.tensor_scalar(xaT[:, :], xT23[:, :], ac[k][:, 0:1], None, ALU.mult).then_inc(xaT_v[k].sem, 1)

            def attend(k, xprev, b):
                dve.wait_ge(s_oev, result_index("C", k, b) + 1)
                dve.reciprocal(rdC[:, k, :], sums[:, k, :]).then_inc(oc_r[k].sem, 1)
                dve.wait_ge(oc_r[k].sem, oc_r[k].upto(b, 1))
                for t in range(NT):
                    dve.scalar_tensor_tensor(out=OC[:, t, :], in0=OC[:, t, :], scalar=rdC[:, k, t:t + 1],
                                             in1=xprev[:, t, :], op0=ALU.mult, op1=ALU.add).then_inc(oc_v[k].sem, 1)

            def half_slot(it, odd, at, now, back1, back2, back3):
                if present(it, 1):
                    b = it - 1
                    if at in (0.5, 1, 1.5):
                        ff_bias(b, int(2 * (at - 0.5)))
                    if at == 1.5:
                        ff_bias(b, 3)
                    if at == 1:
                        make_bias1(b, 1 - odd)
                if present(it, 2) and at == 1.5:
                    group_b(it - 2)
                if present(it, 3) and at == 2.5:
                    b = it - 3
                    attend(1, x3, b)
                    dve.wait_ge(oc_v[1].sem, oc_v[1].upto(b, NT))
                    ln_out.stats(dve, b, OC)
                if present(it, 2) and at == 2.5:
                    dve.wait_ge(cB_v.sem, cB_v.upto(it - 2, 1))
                    ln_x2.stats(dve, it - 2, cB)
                if present(it, -1) and at == 2.5:
                    dve.wait_ge(s_xin, 16 * (it + 2))
                    ln1.stats(dve, it + 1, xin[1 - odd])
                if present(it, 3) and at == 3:
                    if due(n := 16 * (it - 3)):
                        dve.wait_ge(s_out, n)
                    ln_out.scale(dve, it - 3, OC, xo)
                if present(it, 2) and at == 3.5:
                    b = it - 2
                    if due(n := ln_x3.stat.upto(b, 0)):
                        dve.wait_ge(ln_x3.stat.sem, n)
                    if due(n := 16 * b):
                        dve.wait_ge(s_saved, n)
                    ln_x2.scale(dve, b, cB, x2)
                if present(it, 1):
                    b = it - 1
                    if at == 3:
                        mlp_residual(b)
                        dve.wait_ge(s_xfree, x_index("w2", b) + 1)
                        lnf.stats(dve, b, sumx)
                    if at == 4:
                        if due(n := cB_v.upto(b, 0)):
                            dve.wait_ge(cB_v.sem, n)
                        if due(n := previous(x_index("x1T", b - 1) + 1, b)):
                            dve.wait_ge(s_x, n)
                        lnf.scale(dve, b, sumx, x1)
                    if at == 5:
                        projected(b)
                    if at == 5.5:
                        logits(b)
                if present(it, -1) and at == 4:
                    b = it + 1
                    if due(n := q_v.upto(b, 0)):
                        dve.wait_ge(q_v.sem, n)
                    ln1.scale(dve, b, xin[1 - odd], qn)
                if present(it, 2) and at == 7:
                    scaled(0, it - 2)
                if present(it, 0):
                    if at == 7:
                        group_a(it, 0)
                    if at == 10.5:
                        group_a(it, 1)
                    if at == 11.5:
                        dve.wait_ge(cA_v.sem, cA_v.upto(it, 1))
                        ln2.stats(dve, it, xr)
                    if at == 12.5:
                        if due(n := previous(x_index("yT", it - 1) + 1, it)):
                            dve.wait_ge(s_x, n)
                        ln2.scale(dve, it, xr, yn)
                if present(it, 2):
                    b = it - 2
                    if at == 11.5:
                        attend(0, x2, b)
                        dve.wait_ge(oc_v[0].sem, oc_v[0].upto(b, NT))
                        ln_x3.stats(dve, b, OC)
                    if at == 12:
                        ln_x3.scale(dve, b, OC, x3)
                    if at == 13:
                        scaled(1, b)
                if now and at == int(at):
                    mask(now, 0)
                    mask(now, 1)
                elif now:
                    mask(now, 2)
                    mask(now, 3)
                    maxima(now)
            run_iterations(dve, half_slot)

            dve.wait_ge(s_looked, B)
            dve.tensor_reduce(fmax[:, :], flags[:, :], AX.X, ALU.max).then_inc(s_flag, 1)
            dve.wait_ge(s_flag, 3)
            dve.tensor_scalar(flag[:, :], X[0:1, 0:1], 0.0, None, ALU.is_gt).then_inc(s_flag, 1)

            def general_dve(b):
                masks = [hpre[:, m, :].bitcast(i32) for m in range(4)]
                for k in range(2):
                    n = 2 * b + k
                    xk = x2 if k == 0 else x3
                    dve.wait_ge(g_act.sem, g_act.upto(n, 1))
                    for m in range(4):
                        dve.tensor_scalar(Pr[1][:, m, :], xT23[:, :], ac[k][:, m:m + 1], None,
                                          ALU.mult).then_inc(g_dve.sem, 1)
                    dve.wait_ge(s_gload, 16 * 2 * (b + 1))
                    for i in range(NT):
                        row = 4 + 12 * i
                        dve.memset(Y[0][:, i, :], BIG).then_inc(g_dve.sem, 1)
                        dve.wait_ge(g_dve.sem, g_dve.upto(n, row + 1))
                        for m in range(4):
                            dve.tensor_scalar(masks[m], adji[0][:, i, :], float(m + 1), None,
                                              ALU.is_equal).then_inc(g_dve.sem, 1)
                        for m in range(4):
                            own, scored = val(dve, g_dve.upto(n, row + 5 + m)), val(dve, g_pe.upto(n, 2 + i))
                            dve.wait_ge(s_const, 1)
                            dve.wait_ge(g_dve.sem, own)
                            dve.wait_ge(g_pe.sem, scored)
                            dve.copy_predicated(Y[0][:, i, :], masks[m],
                                                T[m // 2][:, N * (m % 2):N * (m % 2 + 1)]).then_inc(g_dve.sem, 1)
                        dve.wait_ge(g_dve.sem, g_dve.upto(n, row + 9))
                        dve.scalar_tensor_tensor(out=Y[0][:, i, :], in0=Y[0][:, i, :], scalar=0.2, in1=Y[0][:, i, :],
                                                 op0=ALU.mult, op1=ALU.max).then_inc(g_dve.sem, 1)
                        dve.wait_ge(g_dve.sem, g_dve.upto(n, row + 10))
                        dve.tensor_reduce(mx[0][:, i:i + 1], Y[0][:, i, :], AX.X, ALU.max).then_inc(g_dve.sem, 1)
                        dve.wait_ge(g_dve.sem, g_dve.upto(n, row + 11))
                        dve.tensor_scalar(nm[0][:, i:i + 1], mx[0][:, i:i + 1], -1.0, None, ALU.mult).then_inc(g_dve.sem, 1)
                    end = 4 + 12 * NT
                    dve.wait_ge(g_act.sem, g_act.upto(n, 4 + NT))
                    dve.reciprocal(rdC[:, 0, :], sums[:, 0, :]).then_inc(g_dve.sem, 1)
                    dve.wait_ge(g_dve.sem, g_dve.upto(n, end + 1))
                    for t in range(NT):
                        dve.scalar_tensor_tensor(out=OC[:, t, :], in0=OC[:, t, :], scalar=rdC[:, 0, t:t + 1],
                                                 in1=xk[:, t, :], op0=ALU.mult, op1=ALU.add).then_inc(g_dve.sem, 1)
                    dve.wait_ge(g_dve.sem, g_dve.upto(n, end + 1 + NT))
                    for t in range(NT):
                        dve.bn_stats(ln_g.st[:, t, :], OC[:, t, :]).then_inc(ln_g.stat.sem, 1)
                    for t in range(NT):
                        got = val(dve, ln_g.stat.upto(n, t + 1))
                        dve.wait_ge(s_const, 1)
                        dve.wait_ge(ln_g.stat.sem, got)
                        dve.bn_aggr(ln_g.mv[:, t, :], ln_g.st[:, t, :]).then_inc(ln_g.stat.sem, 1)
                    ln_g.scale(dve, n, OC, x3 if k == 0 else xo)
            general(dve, general_dve)

        @block.tensor
        def _(pe):
            pe.wait_ge(s_cload, 16 * CONST_LOADS)
            pe.wait_ge(s_const, CONSTS)
            pe.matmul(O[:, 0:2 * H1], wl[:, :], head_a[:, :], start=True, stop=True).then_inc(s_cp, 1)
            pe.matmul(X[0:2 * H1, 0:1], head_a[:, :], blc[:, :], start=True, stop=True).then_inc(s_cp, 1)
            pe.wait_ge(s_cv, 2)

            def scores(u, i):
                if due(n := 4 * u.g + i - 1):
                    pe.wait_ge(s_read, n)
                rows = slice(P * i, P * (i + 1))
                if u.kind == "A":
                    if i == 0 and u.h == 0:
                        pe.wait_ge(s_stack, 16 * STACK_LOADS * (u.b + 1))
                    lhsT, rhs = stL[u.bp][:, u.h, rows], stR[u.bp][:, u.h, :]
                elif u.kind == "B":
                    if i == 0 and u.h == 0:
                        pe.wait_ge(s_lstack, 16 * LSTACK_LOADS * (u.b + 1))
                    lhsT, rhs = st1L[:, u.h, rows], st1R[:, u.h, :]
                else:
                    if i == 0:
                        pe.wait_ge(xaT_v[u.h].sem, xaT_v[u.h].upto(u.b, 1))
                    lhsT, rhs = xaT[:, rows], xT23[:, :]
                pe.matmul(S[i % 2][:, :], lhsT, rhs, start=True, stop=True).then_inc(s_score, 1)

            def transposes(u, half):
                pe.wait_ge(s_exp, 4 * u.g + 2 * half + 2)
                if due(n := 2 * (u.g - 1) + half + 1):
                    pe.wait_ge(s_copied, n)
                for ii in range(2):
                    for j in range(NT):
                        ins = pe.transpose(T[half][:, N * ii + P * j:N * ii + P * (j + 1)],
                                           Pr[u.par][:, 2 * half + ii, P * j:P * (j + 1)], identf[:, :])
                ins.then_inc(s_tr, 1)

            def values(u):
                pe.wait_ge(s_copied, 2 * u.g + 2)
                group = u.h if u.kind == "C" else u.h // GROUP
                if u.kind == "C" or u.h % GROUP == 0:
                    if due(n := result_index(u.kind, group, u.b)):
                        pe.wait_ge(s_oev, n)
                if u.kind == "A" and u.h == 0:
                    pe.wait_ge(q_v.sem, q_v.upto(u.b, 2))
                if u.kind == "C":
                    for i in range(NT):
                        for j in range(NT):
                            ins = pe.matmul(O[:, D * i:D * (i + 1)], PT[u.par][:, i, P * j:P * (j + 1)],
                                            (x2 if u.h == 0 else x3)[:, j, :], start=(j == 0), stop=(j == NT - 1))
                else:
                    at = W0 * (u.h % GROUP)
                    for j in range(NT):
                        V = VA[u.bp][:, j, u.h, :] if u.kind == "A" else VB[:, j, D1 * u.h:D1 * (u.h + 1)]
                        ins = pe.matmul(O[at:at + W0, :], V, PT[u.par][:, :, P * j:P * (j + 1)],
                                        start=(j == 0), stop=(j == NT - 1))
                ins.then_inc(s_pv, 1)

            def turn(name, b, src):
                if due(n := x_index(name, b)):
                    pe.wait_ge(s_xfree, n)
                for t in range(NT):
                    block = src[:, P * t:P * (t + 1)] if name in ("oa0", "oa1", "ob") else src[:, t, :]
                    ins = pe.transpose(X[:, P * t:P * (t + 1)], block, identf[:, :])
                ins.then_inc(s_x, 1)

            def turn_part(b, k):
                pe.wait_ge(q_v.sem, q_v.upto(b, 2 * k + 3))
                if due(n := x_index("q" + "hml"[k], b)):
                    pe.wait_ge(s_xfree, n)
                for t in range(NT):
                    ins = pe.transpose(Xh[:, P * t:P * (t + 1)], QP[:, t, k, :], identh[:, :])
                ins.then_inc(s_x, 1)

            def ff(b, c):
                pe.wait_ge(s_xfree, x_index(f"f{c}", b))
                pe.matmul(X[:, :], w1s[:, P * c:P * (c + 1)], yT[:, :], start=True, stop=True).then_inc(s_x, 1)

            def ff2(b):
                pe.wait_ge(s_xfree, x_index("w2", b))
                pe.wait_ge(gelu_v.sem, gelu_v.upto(b, 1))
                for t in range(NT):
                    for c in range(FC):
                        ins = pe.matmul(X[:, D * t:D * (t + 1)], hpre[:, c, P * t:P * (t + 1)], w2s[:, c, :],
                                        start=(c == 0), stop=(c == FC - 1))
                ins.then_inc(s_x, 1)

            def proj(b):
                pe.wait_ge(s_xfree, x_index("proj", b))
                for t in range(NT):
                    ins = pe.matmul(X[:, D * t:D * (t + 1)], x1T[:, P * t:P * (t + 1)], wlT[:, :], start=True, stop=True)
                ins.then_inc(s_x, 1)

            def logits(b):
                pe.wait_ge(s_xfree, x_index("lsd", b))
                pe.matmul(X[0:2 * H1, :], wa[:, :], x1T[:, :], start=True, stop=True).then_inc(s_x, 1)

            def half_slot(it, odd, at, now, back1, back2, back3):
                if present(it, 1):
                    if at in (0, 0.5, 1, 1.5):
                        ff(it - 1, int(2 * at))
                if present(it, 2) and at == 1.5:
                    pe.wait_ge(s_oev, result_index("B", 0, it - 2) + 1)
                    turn("ob", it - 2, OT[2])
                if present(it, 1):
                    b = it - 1
                    if at == 2.5:
                        ff2(b)
                    if at == 4.5:
                        pe.wait_ge(lnf.done.sem, lnf.done.upto(b, NT))
                        turn("x1T", b, x1)
                    if at == 5:
                        proj(b)
                    if at == 5.5:
                        logits(b)
                if present(it, -1) and at == 6:
                    turn_part(it + 1, 0)
                if present(it, 2) and at == 6.5:
                    pe.wait_ge(ln_x2.done.sem, ln_x2.done.upto(it - 2, NT))
                    turn("xT2", it - 2, x2)
                if present(it, 0) and at == 7:
                    pe.wait_ge(s_oev, result_index("A", 0, it) + 1)
                    turn("oa0", it, OT[0])
                if present(it, -1) and at in (8, 8.5):
                    turn_part(it + 1, int(2 * at - 15))
                if present(it, 0) and at == 10.5:
                    pe.wait_ge(s_oev, result_index("A", 1, it) + 1)
                    turn("oa1", it, OT[1])
                if present(it, 2) and at == 12.5:
                    pe.wait_ge(ln_x3.done.sem, ln_x3.done.upto(it - 2, NT))
                    turn("xT3", it - 2, x3)
                if present(it, 0) and at == 13.5:
                    pe.wait_ge(y_v.sem, y_v.upto(it, 2))
                    turn("yT", it, yn)
                if at == int(at):
                    if now:
                        scores(now, 0)
                        scores(now, 1)
                    if back2:
                        transposes(back2, 0)
                    if now:
                        scores(now, 2)
                    if back3:
                        values(back3)
                else:
                    if back2:
                        transposes(back2, 1)
                    if now:
                        scores(now, 3)
            run_iterations(pe, half_slot)

            pe.wait_ge(s_flag, 2)
            pe.wait_ge(s_xfree, len(X_USES) * B)
            pe.matmul(X[0:1, 0:1], fmax[:, :], ones1[:, :], start=True, stop=True).then_inc(s_flag, 1)

            def general_pe(b):
                for k in range(2):
                    n = 2 * b + k
                    xk = x2 if k == 0 else x3
                    if k == 0:
                        pe.wait_ge(s_gload, 16 * 2 * (b + 1))
                    else:
                        pe.wait_ge(ln_g.done.sem, ln_g.done.upto(n - 1, NT))
                    for t in range(NT):
                        ins = pe.transpose(X[:, P * t:P * (t + 1)], xk[:, t, :], identf[:, :])
                    ins.then_inc(g_pe.sem, 1)
                    for i in range(NT):
                        pe.wait_ge(g_dve.sem, g_dve.upto(n, 4 + 12 * i))
                        for m in range(4):
                            ins = pe.matmul(T[m // 2][:, N * (m % 2):N * (m % 2 + 1)], Pr[1][:, m, P * i:P * (i + 1)],
                                            xT23[:, :], start=True, stop=True)
                        ins.then_inc(g_pe.sem, 1)
                    pe.wait_ge(g_act.sem, g_act.upto(n, 1 + NT))
                    for i in range(NT):
                        for j in range(NT):
                            ins = pe.transpose(T[i // 2][:, N * (i % 2) + P * j:N * (i % 2) + P * (j + 1)],
                                               Pr[0][:, i, P * j:P * (j + 1)], identf[:, :])
                    ins.then_inc(g_pe.sem, 1)
                    pe.wait_ge(g_act.sem, g_act.upto(n, 3 + NT))
                    for i in range(NT):
                        for j in range(NT):
                            ins = pe.matmul(O[:, D * i:D * (i + 1)], Y[1][:, i, P * j:P * (j + 1)], xk[:, j, :],
                                            start=(j == 0), stop=(j == NT - 1))
                    ins.then_inc(g_pe.sem, 1)
            general(pe, general_pe)


_INS = ["x", "adj", "L0_gnn_gamma1", "L0_gnn_beta1", "L0_gnn_gamma2", "L0_gnn_beta2", "L0_gnn_W1", "L0_gnn_b1",
        "L0_gnn_W2", "L0_gnn_b2", "L1_gnn_W", "L1_gnn_WT", "L1_gnn_b", "L1_gnn_a",
        "L2_gnn_a0", "L2_gnn_a1", "L2_gnn_a2", "L2_gnn_a3", "L3_gnn_a_0", "L3_gnn_a_1", "L3_gnn_a_2", "L3_gnn_a_3"]


def kernel(**inputs):
    import numpy as _np
    import concourse.bacc as _bacc
    from concourse import mybir as _mybir
    from concourse.bass_utils import run_bass_kernel_spmd as _run

    nc = _bacc.Bacc("TRN2", target_bir_lowering=False, num_devices=1)
    arrays, aps = {}, []
    for name in _INS:
        if name == "L1_gnn_WT":
            a = _np.ascontiguousarray(_np.asarray(inputs["L1_gnn_W"]).T)
        else:
            a = _np.ascontiguousarray(inputs[name])
        if name.startswith(("L2_", "L3_")):
            a = a.reshape(128, 1)
        arrays[f"in_{name}"] = a
        aps.append(nc.dram_tensor(f"in_{name}", a.shape, _mybir.dt.from_np(a.dtype), kind="ExternalInput").ap())
    out = nc.dram_tensor("out", (16, 512, 128), _mybir.dt.float32, kind="ExternalOutput").ap()
    adj_resnorm_kernel(nc, *aps[:14], aps[14:18], aps[18:22], out)
    r = _run(nc, [arrays], core_ids=[0])
    return r.results[0]["out"]
```

```python
from contextlib import ExitStack


import concourse.bass as bass
from concourse import mybir

fp32 = mybir.dt.float32
bf16 = mybir.dt.bfloat16
fp16 = mybir.dt.float16
i32 = mybir.dt.int32
ALU = mybir.AluOpType
ACT = mybir.ActivationFunctionType
AX = mybir.AxisListType

B, N, D = 16, 512, 128
P = 128
NT = N // P
H0, H1 = 8, 4
D0, D1 = D // H0, D // H1
FF = 4 * D
FC = FF // P
W0 = 32
EPS = 1e-5
BIG = -9e15
TERMS_L = "hhhmml"
TERMS_R = "hmlhmh"
K0 = len(TERMS_L) * D0
STACK_LOADS = 2 * len(TERMS_L)
LSTACK_LOADS = 6
CONST_LOADS = 20 + 2 * H1
CONSTS = 12

ORDER = [("A", 0), ("A", 1), ("A", 2), ("A", 3), ("D", 0), ("A", 4), ("A", 5), ("A", 6), ("A", 7), ("C", 0),
         ("B", 0), ("B", 1), ("B", 2), ("B", 3)]
LAG = {"A": 0, "B": 1, "C": 2, "D": 3}
SLOTS = len(ORDER)
LOOP = (4, B - 2)
GROUP = P // 32
RESULTS = [("A", 0), ("D", 0), ("A", 1), ("C", 0), ("B", 0)]
X_USES = [("yT", 1), ("f0", 1), ("xT3", 3), ("f1", 1), ("f2", 1), ("f3", 1), ("ob", 2), ("w2", 1), ("x1T", 1),
          ("proj", 1), ("lsd", 1), ("qh", -1), ("xT2", 2), ("oa0", 0), ("qm", -1), ("ql", -1), ("oa1", 0)]
X_LAG = dict(X_USES)


def present(it, lag):
    return not isinstance(it, int) or 0 <= it - lag < B


def count_before(it, lags):
    if isinstance(it, int):
        return sum(min(max(it - lag, 0), B) for lag in lags)
    return len(lags) * it - sum(lags)


def index_in(it, lags, n):
    before = sum(1 for lag in lags[:n] if present(it, lag))
    return count_before(it, lags) + before


RING = 3


def behind(it, pos, i):
    bank = (NT * pos + i) % RING
    n, p, k = 0, pos, i
    while True:
        n += 1
        k -= 1
        if k < 0:
            k, p = NT - 1, p - 1
            while True:
                if p < 0:
                    it, p = it - 1, SLOTS - 1
                if isinstance(it, int) and it < -1:
                    return 10 ** 6
                if present(it, LAG[ORDER[p][0]]):
                    break
                p -= 1
        if (NT * p + k) % RING == bank:
            return n


class Unit:

    def __init__(self, it, odd, pos):
        self.kind, self.h = ORDER[pos]
        self.bank = [(NT * pos + i) % RING for i in range(NT)]
        self.behind = [behind(it, pos, i) for i in range(NT)]
        lags = [LAG[k] for k, _ in ORDER]
        self.b = it - LAG[self.kind]
        self.bp = (odd + LAG[self.kind]) % 2
        self.g = index_in(it, lags, pos)
        self.par = self.g % 2 if isinstance(it, int) else (sum(lags) + pos) % 2
        if self.kind != "A":
            leaky = [LAG[k] for k, _ in ORDER if k != "A"]
            self.leaky = index_in(it, leaky, sum(1 for k, _ in ORDER[:pos] if k != "A"))


def due(count):
    return not isinstance(count, int) or count > 0


def val(eng, count):
    return count if isinstance(count, int) else eng.compute_val(count)


class Steps:

    def __init__(self, sem, per):
        self.sem, self.per = sem, per

    def upto(self, b, k):
        return self.per * b + k


def adj_resnorm_kernel(nc, x, adj, gamma1, beta1, gamma2, beta2, W1, b1, W2, b2, Wl1, WTl1, bl1, al1,
                       a2s, a3s, out):
    ctx = ExitStack()
    with ctx:
        def sb(name, shape, dt=fp32):
            return ctx.enter_context(nc.sbuf_tensor(name, shape, dt))

        def sem(name):
            return ctx.enter_context(nc.semaphore(name))

        def steps(name, per):
            return Steps(sem(name), per)

        identf, identh = sb("identf", [P, P]), sb("identh", [P, P], bf16)
        g1b, be1b, g2b, be2b, b2b, bl1b = (sb(n, [P, D]) for n in ("g1b", "be1b", "g2b", "be2b", "b2b", "bl1b"))
        w1s, w2s, b1c = sb("w1s", [P, FF]), sb("w2s", [P, FC, D]), sb("b1c", [P, FC])
        wl, wlT, blc = sb("wl", [P, D]), sb("wlT", [P, D]), sb("blc", [P, 1])
        head_a = sb("head_a", [P, 2 * H1])
        wa, wab = sb("wa", [P, 2 * H1]), sb("wab", [2 * H1, 1])
        ac = [sb("a2c", [P, 4]), sb("a3c", [P, 4])]
        mhalf = sb("mhalf", [P, NT])
        Y = [sb(f"Y{i}", [P, NT, N]) for i in range(2)]
        Pr = [sb(f"Pr{i}", [P, NT, N]) for i in range(2)]
        PT = [sb(f"PT{i}", [P, NT, N]) for i in range(2)]
        mx = [sb(f"mx{i}", [P, NT]) for i in range(2)]
        negmx = [sb(f"negmx{i}", [P, NT]) for i in range(2)]
        nm = [sb(f"nm{i}", [P, NT]) for i in range(2)]
        xin = [sb(f"xin{i}", [P, NT, D]) for i in range(2)]
        adji = [sb(f"adji{i}", [P, NT, N], i32) for i in range(2)]
        bias0 = [sb(f"bias0{i}", [P, NT, N], bf16) for i in range(2)]
        bias1 = [sb(f"bias1{i}", [P, NT, N], bf16) for i in range(2)]
        stL = [sb(f"stL{i}", [K0, H0, N], bf16) for i in range(2)]
        stR = [sb(f"stR{i}", [K0, H0, N], bf16) for i in range(2)]
        qT = {s: sb(f"qT{s}", [P, N], bf16) for s in "hml"}
        QP = sb("QP", [P, NT, 3, D], bf16)
        VA = [sb(f"VA{i}", [P, NT, H0, W0]) for i in range(2)]
        VB = sb("VB", [P, NT, D])
        OT = [sb(f"OT{i}", [P, N]) for i in range(3)]
        OC = sb("OC", [P, NT, D])
        qn = sb("qn", [P, NT, D])
        rdA = sb("rdA", [P, NT, H0])
        xr, yn, yT = sb("xr", [P, NT, D]), sb("yn", [P, NT, D]), sb("yT", [P, N])
        hpre = sb("hpre", [P, FC, N])
        sumx, x1, x1T = sb("sumx", [P, NT, D]), sb("x1", [P, NT, D]), sb("x1T", [P, N])
        lsd = sb("lsd", [2 * H1, N])
        lpart = {s: sb(f"lp{s}", [2 * H1, N], bf16) for s in "hml"}
        st1L, st1R = sb("st1L", [K0, H1, N], bf16), sb("st1R", [K0, H1, N], bf16)
        cB, rdB, x2 = sb("cB", [P, NT, D]), sb("rdB", [P, H1, NT]), sb("x2", [P, NT, D])
        xT23, xaT = sb("xT23", [P, N]), sb("xaT", [P, N])
        sumB = sb("sumB", [P, H1, NT])
        sums, rdC = sb("sums", [P, 2, NT]), sb("rdC", [P, 2, NT])
        x3, xo = sb("x3", [P, NT, D]), sb("xo", [P, NT, D])

        def pb(name, n):
            return ctx.enter_context(nc.psum_tensor(name, [P, n * N], fp32))

        S = [pb(f"S{i}", 1) for i in range(RING)]
        T = [pb(f"T{i}", 1) for i in range(RING)]
        four = S + [T[0]]
        O, X = pb("O", 1), pb("X", 1)
        Xh = X[:, :].bitcast(bf16)[:, 0:N]

        junk, flags = sb("junk", [P, NT, N], bf16), sb("flags", [P, B])
        fmax, ones1, minus1, flag = sb("fmax", [P, 1]), sb("ones1", [P, 1]), sb("minus1", [P, 1]), sb("flag", [1, 1], i32)
        saved = nc.dram_tensor("layer1_result", (B, N, D), fp32, kind="Internal").ap()

        parts_dram = nc.dram_tensor("query_parts", (2, 3, P, N), bf16, kind="Internal").ap()

        s_score = sem("s_score")
        s_read = sem("s_read")
        s_neg = sem("s_neg")
        s_leak = sem("s_leak")
        s_exp = sem("s_exp")
        s_tr = sem("s_tr")
        s_copied = sem("s_copied")
        s_pv = sem("s_pv")
        s_oev = sem("s_oev")
        s_x = sem("s_x")
        s_xfree = sem("s_xfree")
        s_adj, s_xin = sem("s_adj"), sem("s_xin")
        s_cload, s_part, s_stack, s_lstack, s_out = sem("s_cload"), sem("s_part"), sem("s_stack"), sem("s_lstack"), sem("s_out")
        s_saved = sem("s_saved")
        s_looked = sem("s_looked")
        s_flag = sem("s_flag")
        s_const = sem("s_const")
        s_cv = sem("s_cv")
        s_cp = sem("s_cp")
        b0_done, b1_done = steps("b0_done", 1), steps("b1_done", 1)
        q_v = steps("q_v", 7)
        cA_v, cA_r = steps("cA_v", 1), steps("cA_r", 4)
        y_v = steps("y_v", 2)
        gelu_v = steps("gelu_v", 1)
        sum_v = steps("sum_v", 2)
        lp_v = steps("lp_v", 5)
        cB_v, cB_r = steps("cB_v", 1), steps("cB_r", 2)
        xaT_v = [steps("xaT2_v", 1), steps("xaT3_v", 1)]
        oc_r = [steps("oc2_r", 1), steps("oc3_r", 1)]
        oc_v = [steps("oc2_v", NT), steps("oc3_v", NT)]

        g_pe, g_act, g_dve = steps("g_pe", 3 + NT), steps("g_act", 2 + 2 * NT), steps("g_dve", 4 + 12 * NT + 1 + NT)
        s_gload = sem("s_gload")

        class Norm:

            def __init__(self, name):
                self.st, self.mv = sb(name + "_st", [P, NT, 6]), sb(name + "_mv", [P, NT, 2])
                self.ve, self.rs = sb(name + "_ve", [P, NT]), sb(name + "_rs", [P, NT])
                self.stat = steps(name + "_stat", 2 * NT)
                self.root = steps(name + "_root", 2)
                self.done = steps(name + "_done", NT)

            def stats(self, dve, b, src):
                if due(n := self.root.upto(b, 0)):
                    dve.wait_ge(self.root.sem, n)
                for t in range(NT):
                    dve.bn_stats(self.st[:, t, :], src[:, t, :]).then_inc(self.stat.sem, 1)
                for t in range(NT):
                    n = val(dve, self.stat.upto(b, t + 1))
                    dve.wait_ge(s_const, 1)
                    dve.wait_ge(self.stat.sem, n)
                    dve.bn_aggr(self.mv[:, t, :], self.st[:, t, :]).then_inc(self.stat.sem, 1)

            def roots(self, pool, b):
                ready, free = val(pool, self.stat.upto(b, 2 * NT)), val(pool, self.done.upto(b, 0))
                pool.wait_ge(s_const, 1)
                pool.wait_ge(self.stat.sem, ready)
                if due(free):
                    pool.wait_ge(self.done.sem, free)
                pool.tensor_scalar(self.ve[:, :], self.mv[:, :, 1], EPS, None, ALU.add).then_inc(self.root.sem, 1)
                pool.wait_ge(self.root.sem, self.root.upto(b, 1))
                pool.tensor_tensor(self.rs[:, :], self.ve[:, :], mhalf[:, :], ALU.pow).then_inc(self.root.sem, 1)

            def scale(self, dve, b, src, dst):
                dve.wait_ge(self.root.sem, self.root.upto(b, 2))
                for t in range(NT):
                    dve.tensor_scalar(dst[:, t, :], src[:, t, :], self.mv[:, t, 0:1], self.rs[:, t:t + 1],
                                      ALU.subtract, ALU.mult).then_inc(self.done.sem, 1)

        ln1, ln2, lnf, ln_x2, ln_x3, ln_out, ln_g = (
            Norm(name) for name in ("ln1", "ln2", "lnf", "ln_x2", "ln_x3", "ln_out", "ln_g"))

        ctx.enter_context(nc.allow_non_contiguous_dma(reason="columns of a few hundred constants, once"))
        block = ctx.enter_context(nc.Block())

        def general(eng, program, end=None):
            eng.wait_ge(s_flag, 4)
            raised = eng.value_load(flag[0:1, 0:1], min_val=0, max_val=1)
            with eng.If(raised > 0):
                with eng.Fori(0, B) as b:
                    program(b)
                if end:
                    end()

        LAGS = [LAG[k] for k, _ in ORDER]
        POS = {u: p for p, u in enumerate(ORDER)}

        def g_of(kind, h, b):
            return index_in(b + LAG[kind], LAGS, POS[(kind, h)])

        def after(kind, h, b):
            return g_of(kind, h, b) + 1 if not isinstance(b, int) or b >= 0 else 0

        def x_index(name, b):
            names, lags = zip(*X_USES)
            return index_in(b + X_LAG[name], lags, names.index(name))

        def result_index(kind, group, b):
            return index_in(b + LAG[kind], [LAG[k] for k, _ in RESULTS], RESULTS.index((kind, group)))

        def previous(count, b):
            return count if not isinstance(b, int) or b >= 1 else 0

        def run_iterations(eng, half_slot):
            def iteration(it, odd, units):
                for p in range(SLOTS):
                    unit = Unit(it, odd, p) if present(it, LAG[ORDER[p][0]]) else None
                    units = [unit] + units[:3]
                    half_slot(it, odd, p, *units)
                    half_slot(it, odd, p + 0.5, *units)
                return units

            def last_units(it, odd):
                return [Unit(it, odd, SLOTS - 1 - k) for k in range(3)]

            units = [None] * 3
            for it in range(-1, LOOP[0]):
                units = iteration(it, it % 2, units)
            with eng.Fori(*LOOP, 2) as it:
                middle = iteration(it, LOOP[0] % 2, last_units(it - 1, (LOOP[0] - 1) % 2))
                iteration(it + 1, (LOOP[0] + 1) % 2, middle)
            units = last_units(LOOP[1] - 1, (LOOP[1] - 1) % 2)
            for it in range(LOOP[1], B + 4):
                units = iteration(it, it % 2, units)

        def tiles(dram, b):
            return dram[bass.ds(b, 1), :, :].rearrange("a (t p) n -> p (a t) n", p=P)

        @block.sync
        def _(sp):
            def load(dst, src):
                sp.dma_start(dst, src).then_inc(s_cload, 16)

            def row(v):
                return v.rearrange("(a n) -> a n", a=1).broadcast_to([P, D])
            for dst, v in ((g1b, gamma1), (be1b, beta1), (g2b, gamma2), (be2b, beta2), (b2b, b2), (bl1b, bl1)):
                load(dst[:, :], row(v))
            load(w1s[:, :], W1)
            load(w2s[:, :, :], W2.rearrange("(c p) n -> p c n", p=P))
            load(b1c[:, :], b1.rearrange("(c p) -> p c", p=P))
            load(wl[:, :], Wl1)
            load(wlT[:, :], WTl1)
            load(blc[:, :], bl1.rearrange("(p a) -> p a", a=1))
            for c, vs in ((ac[0], a2s), (ac[1], a3s)):
                for k in range(4):
                    load(c[:, k:k + 1], vs[k])
            sp.wait_ge(s_const, 2)
            for h in range(H1):
                for k in range(2):
                    load(head_a[D1 * h:D1 * (h + 1), H1 * k + h:H1 * k + h + 1],
                         al1[h:h + 1, D1 * k:D1 * (k + 1)].rearrange("a p -> p a"))

            def load_adj(b, bp):
                used, looked = val(sp, b1_done.upto(b - 1, 0)), val(sp, b - 1)
                if due(used):
                    sp.wait_ge(b1_done.sem, used)
                if due(looked):
                    sp.wait_ge(s_looked, looked)
                sp.dma_start(adji[bp][:, :, :], tiles(adj, b)).then_inc(s_adj, 16)

            def load_x(b, bp):
                if due(n := sum_v.upto(b - 1, 0)):
                    sp.wait_ge(sum_v.sem, n)
                sp.dma_start(xin[bp][:, :, :], tiles(x, b)).then_inc(s_xin, 16)

            def keep_part(k, b, bp):
                evacuated, read_back = val(sp, x_index("q" + "hml"[k], b) + 1), val(sp, 16 * STACK_LOADS * (b - 1))
                sp.wait_ge(s_xfree, evacuated)
                if due(read_back):
                    sp.wait_ge(s_stack, read_back)
                sp.dma_start(parts_dram[bp, k, :, :], qT["hml"[k]][:, :]).then_inc(s_part, 16)

            def stack(b, bp):
                kept, scored = val(sp, 16 * 3 * (b + 1)), val(sp, 4 * after("A", H0 - 1, b - 2))
                sp.wait_ge(s_part, kept)
                if due(scored):
                    sp.wait_ge(s_score, scored)
                part = parts_dram[bp].rearrange("s (h d) n -> s d h n", d=D0)
                for st, terms in ((stL, TERMS_L), (stR, TERMS_R)):
                    for k, s in enumerate(terms):
                        sp.dma_start(st[bp][D0 * k:D0 * (k + 1), :, :], part["hml".index(s)]).then_inc(s_stack, 16)

            def lstack(b, bp):
                split, scored = val(sp, lp_v.upto(b, 5)), val(sp, previous(4 * after("B", H1 - 1, b - 1), b))
                sp.wait_ge(lp_v.sem, split)
                if due(scored):
                    sp.wait_ge(s_score, scored)
                for k, s in enumerate("hml"):
                    sp.dma_start(st1L[k:k + 1, :, :], lpart[s][0:H1, :]).then_inc(s_lstack, 16)
                    sp.dma_start(st1R[3 + k:4 + k, :, :], lpart[s][H1:2 * H1, :]).then_inc(s_lstack, 16)

            def save(b, bp):
                sp.wait_ge(ln_x2.done.sem, ln_x2.done.upto(b, NT))
                sp.dma_start(tiles(saved, b), x2[:, :, :]).then_inc(s_saved, 16)

            def store(b, bp):
                sp.wait_ge(ln_out.done.sem, ln_out.done.upto(b, NT))
                sp.dma_start(tiles(out, b), xo[:, :, :]).then_inc(s_out, 16)

            def half_slot(it, odd, at, *units):
                if present(it, -1):
                    ahead = it + 1, 1 - odd
                    if at == 0.5:
                        load_x(*ahead)
                    if at == 6:
                        load_adj(*ahead)
                    if at in (7.5, 9.5, 10):
                        keep_part((7.5, 9.5, 10).index(at), *ahead)
                if present(it, 2) and at == 7:
                    save(it - 2, odd)
                if present(it, 1) and at == 8.5:
                    lstack(it - 1, 1 - odd)
                if present(it, 3) and at == 10:
                    store(it - 3, 1 - odd)
                if present(it, -1) and at == 10.5:
                    stack(it + 1, 1 - odd)
            run_iterations(sp, half_slot)
            sp.wait_ge(s_out, 16 * B)
            sp.wait_ge(s_saved, 16 * B)

            def general_sp(b):
                sp.wait_ge(s_out, val(sp, 16 * (b + B)))
                sp.dma_start(x2[:, :, :], tiles(saved, b)).then_inc(s_gload, 16)
                sp.dma_start(adji[0][:, :, :], tiles(adj, b)).then_inc(s_gload, 16)
                sp.wait_ge(ln_g.done.sem, NT * (2 * b + 2))
                sp.dma_start(tiles(out, b), xo[:, :, :]).then_inc(s_out, 16)
            general(sp, general_sp, lambda: sp.wait_ge(s_out, 16 * 2 * B))

        @block.gpsimd
        def _(pool):
            pool.memset(identf[:, :], 0.0).then_inc(s_const, 1)
            pool.memset(head_a[:, :], 0.0).then_inc(s_const, 1)
            pool.memset(identh[:, :], 0.0).then_inc(s_const, 1)
            pool.wait_ge(s_const, 3)
            for m in (identf, identh):
                pool.affine_select(out=m[:, :], in_=m[:, :], compare_op=ALU.not_equal, fill=1.0, base=0,
                                   pattern=[[-1, P]], channel_multiplier=1).then_inc(s_const, 1)
            pool.memset(mhalf[:, :], -0.5).then_inc(s_const, 1)
            for st in (st1L, st1R):
                pool.memset(st[:, :, :], 0.0).then_inc(s_const, 1)
            pool.wait_ge(s_const, 8)
            for st in (st1L, st1R):
                pool.memset(st[0:6, :, :], 1.0).then_inc(s_const, 1)
            for v in VA:
                pool.memset(v[:, :, :, D0:W0], 1.0).then_inc(s_const, 1)
            pool.wait_ge(s_const, CONSTS)
            pool.wait_ge(s_cload, 16 * CONST_LOADS)

            def make_bias0(b, bp):
                arrived, used = val(pool, 16 * (b + 1)), val(pool, 4 * after("A", H0 - 1, b - 2))
                pool.wait_ge(s_const, 1)
                pool.wait_ge(s_adj, arrived)
                if due(used):
                    pool.wait_ge(s_read, used)
                pool.tensor_scalar(bias0[bp][:, :, :], adji[bp][:, :, :], 0.0, BIG, ALU.is_le,
                                   ALU.mult).then_inc(b0_done.sem, 1)

            def round_off(v, b, k, part, left, src):
                n = val(pool, v.upto(b, k - 1))
                pool.wait_ge(s_const, 1)
                pool.wait_ge(v.sem, n)
                pool.tensor_copy(part, src).then_inc(v.sem, 1)
                pool.wait_ge(v.sem, v.upto(b, k))
                pool.tensor_tensor(left, src, part, ALU.subtract).then_inc(v.sem, 1)

            def bc(t):
                return t[:, :].rearrange("p (a d) -> p a d", a=1).broadcast_to([P, NT, D])

            def q_affine(b, bp):
                pool.wait_ge(ln1.done.sem, ln1.done.upto(b, NT))
                pool.tensor_tensor(qn[:, :, :], qn[:, :, :], bc(g1b), ALU.mult).then_inc(q_v.sem, 1)
                product, used = val(pool, q_v.upto(b, 1)), val(pool, after("A", H0 - 1, b - 2))
                pool.wait_ge(q_v.sem, product)
                if due(used):
                    pool.wait_ge(s_pv, used)
                heads = lambda m: m.rearrange("p t (h d) -> p t h d", h=H0)
                pool.tensor_tensor(VA[bp][:, :, :, 0:D0], heads(qn[:, :, :]), heads(bc(be1b)), ALU.add).then_inc(q_v.sem, 1)

            def q_part(b, bp, k):
                heads = lambda m: m.rearrange("p t (h d) -> p t h d", h=H0)
                part = QP[:, :, k, :]
                if k == 0:
                    read = val(pool, previous(x_index("ql", b - 1) + 1, b))
                    if due(read):
                        pool.wait_ge(s_x, read)
                    round_off(q_v, b, 3, heads(part), heads(qn[:, :, :]), VA[bp][:, :, :, 0:D0])
                if k == 1:
                    round_off(q_v, b, 5, part, qn[:, :, :], qn[:, :, :])
                if k == 2:
                    n = val(pool, q_v.upto(b, 6))
                    pool.wait_ge(s_const, 1)
                    pool.wait_ge(q_v.sem, n)
                    pool.tensor_copy(part, qn[:, :, :]).then_inc(q_v.sem, 1)

            def combine_a(b, bp):
                pool.wait_ge(cA_r.sem, cA_r.upto(b, 4))
                pool.tensor_tensor(xr[:, :, :], xr[:, :, :], xin[bp][:, :, :], ALU.add).then_inc(cA_v.sem, 1)

            def combine_b(b):
                pool.wait_ge(cB_r.sem, cB_r.upto(b, 2))
                pool.tensor_tensor(cB[:, :, :], cB[:, :, :], x1[:, :, :], ALU.add).then_inc(cB_v.sem, 1)

            def y_affine(b, bp):
                pool.wait_ge(ln2.done.sem, ln2.done.upto(b, NT))
                pool.tensor_tensor(yn[:, :, :], yn[:, :, :], bc(g2b), ALU.mult).then_inc(y_v.sem, 1)
                pool.wait_ge(y_v.sem, y_v.upto(b, 1))
                pool.tensor_tensor(yn[:, :, :], yn[:, :, :], bc(be2b), ALU.add).then_inc(y_v.sem, 1)

            def add_up(b, bp):
                if due(n := lnf.done.upto(b, 0)):
                    pool.wait_ge(lnf.done.sem, n)
                pool.tensor_tensor(sumx[:, :, :], xr[:, :, :], bc(b2b), ALU.add).then_inc(sum_v.sem, 1)
                pool.wait_ge(sum_v.sem, sum_v.upto(b, 1))
                pool.tensor_tensor(sumx[:, :, :], sumx[:, :, :], xin[bp][:, :, :], ALU.add).then_inc(sum_v.sem, 1)

            def l_parts(b):
                rows, free = val(pool, x_index("lsd", b) + 1), val(pool, 16 * LSTACK_LOADS * b)
                pool.wait_ge(s_const, 1)
                pool.wait_ge(s_xfree, rows)
                if due(free):
                    pool.wait_ge(s_lstack, free)
                pool.tensor_copy(lpart["h"][:, :], lsd[:, :]).then_inc(lp_v.sem, 1)
                pool.wait_ge(lp_v.sem, lp_v.upto(b, 1))
                pool.tensor_tensor(lsd[:, :], lsd[:, :], lpart["h"][:, :], ALU.subtract).then_inc(lp_v.sem, 1)
                round_off(lp_v, b, 3, lpart["m"][:, :], lsd[:, :], lsd[:, :])
                n = val(pool, lp_v.upto(b, 4))
                pool.wait_ge(s_const, 1)
                pool.wait_ge(lp_v.sem, n)
                pool.tensor_copy(lpart["l"][:, :], lsd[:, :]).then_inc(lp_v.sem, 1)

            def half_slot(it, odd, at, *units):
                if present(it, 1) and at == 0.5:
                    add_up(it - 1, 1 - odd)
                if present(it, -1):
                    if at == 2:
                        ln1.roots(pool, it + 1)
                    if at == 3:
                        q_affine(it + 1, 1 - odd)
                if present(it, 2):
                    if at == 3.5:
                        combine_b(it - 2)
                    if at == 4:
                        ln_x2.roots(pool, it - 2)
                if present(it, 1) and at == 4.5:
                    lnf.roots(pool, it - 1)
                if present(it, -1) and at in (4, 5, 5.5):
                    q_part(it + 1, 1 - odd, (4, 5, 5.5).index(at))
                if present(it, 1) and at == 6.5:
                    l_parts(it - 1)
                if present(it, 3) and at == 8.5:
                    ln_out.roots(pool, it - 3)
                if present(it, -1) and at == 9:
                    make_bias0(it + 1, 1 - odd)
                if present(it, 0):
                    if at == 12:
                        combine_a(it, odd)
                    if at == 12.5:
                        ln2.roots(pool, it)
                if present(it, 2) and at == 13:
                    ln_x3.roots(pool, it - 2)
                if present(it, 0) and at == 13.5:
                    y_affine(it, odd)
            run_iterations(pool, half_slot)

            def general_pool(b):
                for k in range(2):
                    n = 2 * b + k
                    ready = val(pool, ln_g.stat.upto(n, 2 * NT))
                    pool.wait_ge(s_const, 1)
                    pool.wait_ge(ln_g.stat.sem, ready)
                    pool.tensor_scalar(ln_g.ve[:, :], ln_g.mv[:, :, 1], EPS, None, ALU.add).then_inc(ln_g.root.sem, 1)
                    pool.wait_ge(ln_g.root.sem, ln_g.root.upto(n, 1))
                    pool.tensor_tensor(ln_g.rs[:, :], ln_g.ve[:, :], mhalf[:, :], ALU.pow).then_inc(ln_g.root.sem, 1)
            general(pool, general_pool)

        @block.scalar
        def _(act):
            act.wait_ge(s_cv, 4)

            def exp_guards(u):
                if u.kind == "A":
                    act.wait_ge(s_neg, u.g + 1)
                else:
                    act.wait_ge(s_leak, u.leaky + 1)
                if due(n := 4 * (u.g - 1)):
                    act.wait_ge(s_tr, n)
                used = {"B": cB_r, "C": oc_r[0], "D": oc_r[1]}.get(u.kind)
                if used and due(n := used.upto(u.b, 0)):
                    act.wait_ge(used.sem, n)

            def exp(u, i):
                more = {}
                if u.kind == "B":
                    more = {"accum_out": sumB[:, u.h, i:i + 1]}
                elif u.kind in "CD":
                    more = {"accum_out": sums[:, "CD".index(u.kind), i:i + 1]}
                act.activation(Pr[u.par][:, i, :], Y[u.par][:, i, :], ACT.Exp, bias=nm[u.par][:, i:i + 1],
                               scale=D0 ** -0.5 if u.kind == "A" else 1.0, **more).then_inc(s_exp, 1)

            def copy(u, i):
                if i == 0 and due(n := u.g - 1):
                    act.wait_ge(s_pv, n)
                act.wait_ge(s_tr, 4 * u.g + i + 1)
                act.activation(PT[u.par][:, i, :], T[u.bank[i]][:, :], ACT.Copy).then_inc(s_copied, 1)

            def result(u):
                if u.kind in "CD":
                    norm, b = (ln_out, u.b) if u.kind == "C" else (ln_x3, u.b + 1)
                    if due(n := norm.done.upto(b, 0)):
                        act.wait_ge(norm.done.sem, n)
                    act.wait_ge(s_pv, u.g + 1)
                    act.activation(OC[:, :, :], O[:, :].rearrange("p (t c) -> p t c", t=NT), ACT.Copy).then_inc(s_oev, 1)
                elif u.h % GROUP == GROUP - 1:
                    name = f"oa{u.h // GROUP}" if u.kind == "A" else "ob"
                    if due(n := previous(x_index(name, u.b - 1) + 1, u.b)):
                        act.wait_ge(s_x, n)
                    act.wait_ge(s_pv, u.g + 1)
                    ot = OT[u.h // GROUP if u.kind == "A" else 2]
                    act.activation(ot[:, :], O[:, :], ACT.Copy).then_inc(s_oev, 1)

            def evacuate(name, b, dst, src):
                act.wait_ge(s_x, x_index(name, b) + 1)
                act.activation(dst, src, ACT.Copy).then_inc(s_xfree, 1)

            def gelu(b):
                act.wait_ge(s_xfree, x_index("f3", b) + 1)
                act.activation(hpre[:, :, :], hpre[:, :, :], ACT.Gelu).then_inc(gelu_v.sem, 1)

            def look(b, bp):
                act.wait_ge(s_adj, 16 * (b + 1))
                act.activation(junk[:, :, :], adji[bp][:, :, :], ACT.Relu, bias=minus1[:, 0:1],
                               accum_out=flags[:, bass.ds(b, 1)]).then_inc(s_looked, 1)

            def half_slot(it, odd, at, now, back1, back2, back3):
                if present(it, 1) and at == 0.5:
                    evacuate("yT", it - 1, yT[:, :], X[:, :])
                if present(it, 3) and at == 1.5:
                    evacuate("xT3", it - 3, xT23[:, :], X[:, :])
                if present(it, 1):
                    if at == 3:
                        gelu(it - 1)
                    if at == 5.5:
                        evacuate("x1T", it - 1, x1T[:, :], X[:, :])
                if present(it, -1) and at in (7, 9, 9.5):
                    k = (7, 9, 9.5).index(at)
                    if due(n := 16 * (3 * it + 3)):
                        act.wait_ge(s_part, n)
                    evacuate("q" + "hml"[k], it + 1, qT["hml"[k]][:, :], Xh)
                if present(it, 2) and at == 7.5:
                    evacuate("xT2", it - 2, xT23[:, :], X[:, :])
                if present(it, -1) and at == 12:
                    look(it + 1, 1 - odd)
                if at == int(at) and back1:
                    exp_guards(back1)
                if at > int(at) and back3:
                    result(back3)
                for i in (0, 1) if at == int(at) else (2, 3):
                    if back1:
                        exp(back1, i)
                    if back2:
                        copy(back2, i)
            run_iterations(act, half_slot)

            def general_act(b):
                for k in range(2):
                    n = 2 * b + k
                    act.wait_ge(g_pe.sem, g_pe.upto(n, 1))
                    act.activation(xT23[:, :], X[:, :], ACT.Copy).then_inc(g_act.sem, 1)
                    act.wait_ge(g_dve.sem, g_dve.upto(n, 4 + 12 * NT))
                    for i in range(NT):
                        act.activation(Pr[0][:, i, :], Y[0][:, i, :], ACT.Exp, bias=nm[0][:, i:i + 1],
                                       accum_out=sums[:, 0, i:i + 1]).then_inc(g_act.sem, 1)
                    act.wait_ge(g_pe.sem, g_pe.upto(n, 2 + NT))
                    for i in range(NT):
                        act.activation(Y[1][:, i, :], four[i][:, :], ACT.Copy).then_inc(g_act.sem, 1)
                    act.wait_ge(g_pe.sem, g_pe.upto(n, 3 + NT))
                    act.activation(OC[:, :, :], O[:, :].rearrange("p (t c) -> p t c", t=NT), ACT.Copy).then_inc(g_act.sem, 1)
            general(act, general_act)

        @block.vector
        def _(dve):
            dve.wait_ge(s_cp, 2)
            dve.tensor_copy(wa[:, :], O[:, 0:2 * H1]).then_inc(s_cv, 1)
            dve.tensor_copy(wab[:, :], X[0:2 * H1, 0:1]).then_inc(s_cv, 1)
            dve.wait_ge(s_const, CONSTS)
            dve.wait_ge(s_cload, 16 * CONST_LOADS)
            dve.sem_inc(s_cv, 1)
            dve.memset(minus1[:, :], -1.0).then_inc(s_cv, 1)
            dve.memset(ones1[:, :], 1.0).then_inc(s_flag, 1)

            def mask(u, i):
                scored, left = val(dve, 4 * u.g + i + 1), val(dve, 4 * (u.g - 1))
                bias, made = (bias0, b0_done) if u.kind == "A" else (bias1, b1_done)
                biased = val(dve, made.upto(u.b, 1))
                dve.wait_ge(s_const, 1)
                dve.wait_ge(s_score, scored)
                if i == 0:
                    if due(left):
                        dve.wait_ge(s_exp, left)
                    dve.wait_ge(made.sem, biased)
                dve.tensor_tensor_reduce(out=Y[u.par][:, i, :], in0=S[u.bank[i]][:, :], in1=bias[u.bp][:, i, :], scale=1.0,
                                         scalar=-3e38, op0=ALU.add, op1=ALU.max,
                                         accum_out=mx[u.par][:, i:i + 1]).then_inc(s_read, 1)

            def maxima(u):
                p = u.par
                dve.wait_ge(s_read, 4 * u.g + 4)
                if u.kind == "A":
                    dve.tensor_scalar(nm[p][:, :], mx[p][:, :], -D0 ** -0.5, None, ALU.mult).then_inc(s_neg, 1)
                    return
                dve.tensor_scalar(negmx[p][:, :], mx[p][:, :], -1.0, None, ALU.mult).then_inc(s_neg, 1)
                dve.scalar_tensor_tensor(out=Y[p][:, :, :], in0=Y[p][:, :, :], scalar=0.2, in1=Y[p][:, :, :],
                                         op0=ALU.mult, op1=ALU.max)
                dve.wait_ge(s_neg, u.g + 1)
                dve.scalar_tensor_tensor(out=nm[p][:, :], in0=mx[p][:, :], scalar=-0.2, in1=negmx[p][:, :],
                                         op0=ALU.mult, op1=ALU.min).then_inc(s_leak, 1)

            def make_bias1(b, bp):
                dve.wait_ge(s_adj, 16 * (b + 1))
                dve.wait_ge(b0_done.sem, b0_done.upto(b, 1))
                dve.tensor_scalar(bias1[bp][:, :, :], adji[bp][:, :, :], 1.0, BIG, ALU.not_equal,
                                  ALU.mult).then_inc(b1_done.sem, 1)

            def group_a(b, k):
                heads = X[:, :].rearrange("p (t h d) -> p t h d", t=NT, h=GROUP)
                mine = slice(GROUP * k, GROUP * (k + 1))
                if k == 0 and due(n := sum_v.upto(b, 0)):
                    dve.wait_ge(sum_v.sem, n)
                dve.wait_ge(s_x, x_index(f"oa{k}", b) + 1)
                dve.reciprocal(rdA[:, :, mine], heads[:, :, :, D0]).then_inc(cA_r.sem, 1)
                dve.wait_ge(cA_r.sem, cA_r.upto(b, 2 * k + 1))
                over = rdA[:, :, mine].rearrange("p t (h a) -> p t h a", a=1).broadcast_to([P, NT, GROUP, D0])
                dst = xr[:, :, D0 * GROUP * k:D0 * GROUP * (k + 1)].rearrange("p t (h d) -> p t h d", h=GROUP)
                dve.tensor_tensor(dst, heads[:, :, :, 0:D0], over, ALU.mult).then_inc(cA_r.sem, 1)
                dve.wait_ge(cA_r.sem, cA_r.upto(b, 2 * k + 2))
                dve.sem_inc(s_xfree, 1)

            def group_b(b):
                dve.wait_ge(s_x, x_index("ob", b) + 1)
                dve.reciprocal(rdB[:, :, :], sumB[:, :, :]).then_inc(cB_r.sem, 1)
                if due(n := ln_x2.done.upto(b, 0)):
                    dve.wait_ge(ln_x2.done.sem, n)
                dve.wait_ge(cB_r.sem, cB_r.upto(b, 1))
                over = rdB[:, :, :].rearrange("p h (t a) -> p h t a", a=1).broadcast_to([P, H1, NT, D1])
                dst = cB[:, :, :].rearrange("p t (h d) -> p h t d", h=H1)
                src = X[:, :].rearrange("p (t h d) -> p h t d", t=NT, h=H1)
                dve.tensor_tensor(dst, src, over, ALU.mult).then_inc(cB_r.sem, 1)
                dve.wait_ge(cB_r.sem, cB_r.upto(b, 2))
                dve.sem_inc(s_xfree, 1)

            def ff_bias(b, c):
                dve.wait_ge(s_x, x_index(f"f{c}", b) + 1)
                dve.tensor_scalar(hpre[:, c, :], X[:, :], b1c[:, c:c + 1], None, ALU.add).then_inc(s_xfree, 1)

            def mlp_residual(b):
                dve.wait_ge(sum_v.sem, sum_v.upto(b, 2))
                dve.wait_ge(s_x, x_index("w2", b) + 1)
                dve.tensor_tensor(sumx[:, :, :], X[:, :].rearrange("p (t d) -> p t d", t=NT), sumx[:, :, :],
                                  ALU.add).then_inc(s_xfree, 1)

            def projected(b):
                if due(n := previous(after("B", H1 - 1, b - 1), b)):
                    dve.wait_ge(s_pv, n)
                dve.wait_ge(s_x, x_index("proj", b) + 1)
                bias = bl1b[:, :].rearrange("p (a d) -> p a d", a=1).broadcast_to([P, NT, D])
                dve.tensor_tensor(VB[:, :, :], X[:, :].rearrange("p (t d) -> p t d", t=NT), bias,
                                  ALU.add).then_inc(s_xfree, 1)

            def logits(b):
                if due(n := lp_v.upto(b, 0)):
                    dve.wait_ge(lp_v.sem, n)
                dve.wait_ge(s_x, x_index("lsd", b) + 1)
                dve.tensor_scalar(lsd[:, :], X[0:2 * H1, :], wab[:, 0:1], None, ALU.add).then_inc(s_xfree, 1)

            def scaled(k, b):
                dve.wait_ge(s_xfree, x_index(f"xT{k + 2}", b) + 1)
                dve.tensor_scalar(xaT[:, :], xT23[:, :], ac[k][:, 0:1], None, ALU.mult).then_inc(xaT_v[k].sem, 1)

            def attend(k, xprev, b):
                dve.wait_ge(s_oev, result_index("CD"[k], 0, b) + 1)
                dve.reciprocal(rdC[:, k, :], sums[:, k, :]).then_inc(oc_r[k].sem, 1)
                dve.wait_ge(oc_r[k].sem, oc_r[k].upto(b, 1))
                for t in range(NT):
                    dve.scalar_tensor_tensor(out=OC[:, t, :], in0=OC[:, t, :], scalar=rdC[:, k, t:t + 1],
                                             in1=xprev[:, t, :], op0=ALU.mult, op1=ALU.add).then_inc(oc_v[k].sem, 1)

            def half_slot(it, odd, at, now, back1, back2, back3):
                if present(it, 1) and at in (1.5, 2, 2.5, 3):
                    ff_bias(it - 1, int(2 * (at - 1.5)))
                if present(it, 3):
                    b = it - 3
                    if at == 0.5:
                        ln_x3.scale(dve, b, OC, x3)
                    if at == 2:
                        scaled(1, b)
                    if at == 8.5:
                        attend(1, x3, b)
                        dve.wait_ge(oc_v[1].sem, oc_v[1].upto(b, NT))
                        ln_out.stats(dve, b, OC)
                    if at == 9.5:
                        if due(n := 16 * b):
                            dve.wait_ge(s_out, n)
                        ln_out.scale(dve, b, OC, xo)
                if present(it, -1):
                    b = it + 1
                    if at == 2:
                        dve.wait_ge(s_xin, 16 * (b + 1))
                        ln1.stats(dve, b, xin[1 - odd])
                    if at == 3.5:
                        if due(n := q_v.upto(b, 0)):
                            dve.wait_ge(q_v.sem, n)
                        ln1.scale(dve, b, xin[1 - odd], qn)
                if present(it, 2):
                    b = it - 2
                    if at == 3.5:
                        group_b(b)
                    if at == 4:
                        dve.wait_ge(cB_v.sem, cB_v.upto(b, 1))
                        ln_x2.stats(dve, b, cB)
                    if at == 6.5:
                        if due(n := ln_x3.stat.upto(b, 0)):
                            dve.wait_ge(ln_x3.stat.sem, n)
                        if due(n := 16 * b):
                            dve.wait_ge(s_saved, n)
                        ln_x2.scale(dve, b, cB, x2)
                    if at == 8:
                        scaled(0, b)
                if present(it, 1):
                    b = it - 1
                    if at == 4.5:
                        mlp_residual(b)
                        dve.wait_ge(s_xfree, x_index("w2", b) + 1)
                        lnf.stats(dve, b, sumx)
                    if at == 5.5:
                        if due(n := cB_v.upto(b, 0)):
                            dve.wait_ge(cB_v.sem, n)
                        if due(n := previous(x_index("x1T", b - 1) + 1, b)):
                            dve.wait_ge(s_x, n)
                        lnf.scale(dve, b, sumx, x1)
                        make_bias1(b, 1 - odd)
                    if at == 6:
                        projected(b)
                    if at == 6.5:
                        logits(b)
                if present(it, 0):
                    if at == 8:
                        group_a(it, 0)
                    if at == 12:
                        group_a(it, 1)
                    if at == 12.5:
                        dve.wait_ge(cA_v.sem, cA_v.upto(it, 1))
                        ln2.stats(dve, it, xr)
                    if at == 13.5:
                        if due(n := previous(x_index("yT", it - 1) + 1, it)):
                            dve.wait_ge(s_x, n)
                        ln2.scale(dve, it, xr, yn)
                if present(it, 2) and at == 13:
                    attend(0, x2, it - 2)
                    dve.wait_ge(oc_v[0].sem, oc_v[0].upto(it - 2, NT))
                    ln_x3.stats(dve, it - 2, OC)
                if now and at == int(at):
                    mask(now, 0)
                    mask(now, 1)
                elif now:
                    mask(now, 2)
                    mask(now, 3)
                    maxima(now)
            run_iterations(dve, half_slot)

            dve.wait_ge(s_looked, B)
            dve.tensor_reduce(fmax[:, :], flags[:, :], AX.X, ALU.max).then_inc(s_flag, 1)
            dve.wait_ge(s_flag, 3)
            dve.tensor_scalar(flag[:, :], X[0:1, 0:1], 0.0, None, ALU.is_gt).then_inc(s_flag, 1)

            def general_dve(b):
                masks = [hpre[:, m, :].bitcast(i32) for m in range(4)]
                for k in range(2):
                    n = 2 * b + k
                    xk = x2 if k == 0 else x3
                    dve.wait_ge(g_act.sem, g_act.upto(n, 1))
                    for m in range(4):
                        dve.tensor_scalar(Pr[1][:, m, :], xT23[:, :], ac[k][:, m:m + 1], None,
                                          ALU.mult).then_inc(g_dve.sem, 1)
                    dve.wait_ge(s_gload, 16 * 2 * (b + 1))
                    for i in range(NT):
                        row = 4 + 12 * i
                        dve.memset(Y[0][:, i, :], BIG).then_inc(g_dve.sem, 1)
                        dve.wait_ge(g_dve.sem, g_dve.upto(n, row + 1))
                        for m in range(4):
                            dve.tensor_scalar(masks[m], adji[0][:, i, :], float(m + 1), None,
                                              ALU.is_equal).then_inc(g_dve.sem, 1)
                        for m in range(4):
                            own, scored = val(dve, g_dve.upto(n, row + 5 + m)), val(dve, g_pe.upto(n, 2 + i))
                            dve.wait_ge(s_const, 1)
                            dve.wait_ge(g_dve.sem, own)
                            dve.wait_ge(g_pe.sem, scored)
                            dve.copy_predicated(Y[0][:, i, :], masks[m],
                                                four[m][:, :]).then_inc(g_dve.sem, 1)
                        dve.wait_ge(g_dve.sem, g_dve.upto(n, row + 9))
                        dve.scalar_tensor_tensor(out=Y[0][:, i, :], in0=Y[0][:, i, :], scalar=0.2, in1=Y[0][:, i, :],
                                                 op0=ALU.mult, op1=ALU.max).then_inc(g_dve.sem, 1)
                        dve.wait_ge(g_dve.sem, g_dve.upto(n, row + 10))
                        dve.tensor_reduce(mx[0][:, i:i + 1], Y[0][:, i, :], AX.X, ALU.max).then_inc(g_dve.sem, 1)
                        dve.wait_ge(g_dve.sem, g_dve.upto(n, row + 11))
                        dve.tensor_scalar(nm[0][:, i:i + 1], mx[0][:, i:i + 1], -1.0, None, ALU.mult).then_inc(g_dve.sem, 1)
                    end = 4 + 12 * NT
                    dve.wait_ge(g_act.sem, g_act.upto(n, 2 + 2 * NT))
                    dve.reciprocal(rdC[:, 0, :], sums[:, 0, :]).then_inc(g_dve.sem, 1)
                    dve.wait_ge(g_dve.sem, g_dve.upto(n, end + 1))
                    for t in range(NT):
                        dve.scalar_tensor_tensor(out=OC[:, t, :], in0=OC[:, t, :], scalar=rdC[:, 0, t:t + 1],
                                                 in1=xk[:, t, :], op0=ALU.mult, op1=ALU.add).then_inc(g_dve.sem, 1)
                    dve.wait_ge(g_dve.sem, g_dve.upto(n, end + 1 + NT))
                    for t in range(NT):
                        dve.bn_stats(ln_g.st[:, t, :], OC[:, t, :]).then_inc(ln_g.stat.sem, 1)
                    for t in range(NT):
                        got = val(dve, ln_g.stat.upto(n, t + 1))
                        dve.wait_ge(s_const, 1)
                        dve.wait_ge(ln_g.stat.sem, got)
                        dve.bn_aggr(ln_g.mv[:, t, :], ln_g.st[:, t, :]).then_inc(ln_g.stat.sem, 1)
                    ln_g.scale(dve, n, OC, x3 if k == 0 else xo)
            general(dve, general_dve)

        @block.tensor
        def _(pe):
            pe.wait_ge(s_cload, 16 * CONST_LOADS)
            pe.wait_ge(s_const, CONSTS)
            pe.matmul(O[:, 0:2 * H1], wl[:, :], head_a[:, :], start=True, stop=True).then_inc(s_cp, 1)
            pe.matmul(X[0:2 * H1, 0:1], head_a[:, :], blc[:, :], start=True, stop=True).then_inc(s_cp, 1)
            pe.wait_ge(s_cv, 2)

            def scores(u, i):
                if due(n := 4 * u.g + i + 1 - u.behind[i]):
                    pe.wait_ge(s_read, n)
                rows = slice(P * i, P * (i + 1))
                if u.kind == "A":
                    if i == 0 and u.h == 0:
                        pe.wait_ge(s_stack, 16 * STACK_LOADS * (u.b + 1))
                    lhsT, rhs = stL[u.bp][:, u.h, rows], stR[u.bp][:, u.h, :]
                elif u.kind == "B":
                    if i == 0 and u.h == 0:
                        pe.wait_ge(s_lstack, 16 * LSTACK_LOADS * (u.b + 1))
                    lhsT, rhs = st1L[:, u.h, rows], st1R[:, u.h, :]
                else:
                    if i == 0:
                        scaled = xaT_v["CD".index(u.kind)]
                        pe.wait_ge(scaled.sem, scaled.upto(u.b, 1))
                    lhsT, rhs = xaT[:, rows], xT23[:, :]
                pe.matmul(S[u.bank[i]][:, :], lhsT, rhs, start=True, stop=True).then_inc(s_score, 1)

            def transposes(u, i):
                pe.wait_ge(s_exp, 4 * u.g + i + 1)
                if due(n := 4 * u.g + i + 1 - u.behind[i]):
                    pe.wait_ge(s_copied, n)
                for j in range(NT):
                    ins = pe.transpose(T[u.bank[i]][:, P * j:P * (j + 1)], Pr[u.par][:, i, P * j:P * (j + 1)], identf[:, :])
                ins.then_inc(s_tr, 1)

            def values(u, half):
                if half == 0:
                    if u.h % GROUP == 0 and due(n := result_index(u.kind, u.h // GROUP, u.b)):
                        pe.wait_ge(s_oev, n)
                    if u.kind == "A" and u.h == 0:
                        pe.wait_ge(q_v.sem, q_v.upto(u.b, 2))
                    pe.wait_ge(s_copied, 4 * u.g + NT)
                mine = range(2 * half, 2 * half + 2)
                if u.kind in "CD":
                    for i in mine:
                        for j in range(NT):
                            ins = pe.matmul(O[:, D * i:D * (i + 1)], PT[u.par][:, i, P * j:P * (j + 1)],
                                            (x2 if u.kind == "C" else x3)[:, j, :], start=(j == 0), stop=(j == NT - 1))
                else:
                    at = W0 * (u.h % GROUP)
                    for j in mine:
                        V = VA[u.bp][:, j, u.h, :] if u.kind == "A" else VB[:, j, D1 * u.h:D1 * (u.h + 1)]
                        ins = pe.matmul(O[at:at + W0, :], V, PT[u.par][:, :, P * j:P * (j + 1)],
                                        start=(j == 0), stop=(j == NT - 1))
                if half == 1:
                    ins.then_inc(s_pv, 1)

            def turn(name, b, src):
                if due(n := x_index(name, b)):
                    pe.wait_ge(s_xfree, n)
                for t in range(NT):
                    block = src[:, P * t:P * (t + 1)] if name in ("oa0", "oa1", "ob") else src[:, t, :]
                    ins = pe.transpose(X[:, P * t:P * (t + 1)], block, identf[:, :])
                ins.then_inc(s_x, 1)

            def turn_part(b, k):
                pe.wait_ge(q_v.sem, q_v.upto(b, 2 * k + 3))
                if due(n := x_index("q" + "hml"[k], b)):
                    pe.wait_ge(s_xfree, n)
                for t in range(NT):
                    ins = pe.transpose(Xh[:, P * t:P * (t + 1)], QP[:, t, k, :], identh[:, :])
                ins.then_inc(s_x, 1)

            def ff(b, c):
                pe.wait_ge(s_xfree, x_index(f"f{c}", b))
                pe.matmul(X[:, :], w1s[:, P * c:P * (c + 1)], yT[:, :], start=True, stop=True).then_inc(s_x, 1)

            def ff2(b):
                pe.wait_ge(s_xfree, x_index("w2", b))
                pe.wait_ge(gelu_v.sem, gelu_v.upto(b, 1))
                for t in range(NT):
                    for c in range(FC):
                        ins = pe.matmul(X[:, D * t:D * (t + 1)], hpre[:, c, P * t:P * (t + 1)], w2s[:, c, :],
                                        start=(c == 0), stop=(c == FC - 1))
                ins.then_inc(s_x, 1)

            def proj(b):
                pe.wait_ge(s_xfree, x_index("proj", b))
                for t in range(NT):
                    ins = pe.matmul(X[:, D * t:D * (t + 1)], x1T[:, P * t:P * (t + 1)], wlT[:, :], start=True, stop=True)
                ins.then_inc(s_x, 1)

            def logits(b):
                pe.wait_ge(s_xfree, x_index("lsd", b))
                pe.matmul(X[0:2 * H1, :], wa[:, :], x1T[:, :], start=True, stop=True).then_inc(s_x, 1)

            def half_slot(it, odd, at, now, back1, back2, back3):
                if present(it, 1):
                    if at == 0.5:
                        pe.wait_ge(y_v.sem, y_v.upto(it - 1, 2))
                        turn("yT", it - 1, yn)
                    if at == 1:
                        ff(it - 1, 0)
                if present(it, 3) and at == 1.5:
                    pe.wait_ge(ln_x3.done.sem, ln_x3.done.upto(it - 3, NT))
                    turn("xT3", it - 3, x3)
                if present(it, 1) and at in (1.5, 2, 2.5):
                    ff(it - 1, int(2 * (at - 1)))
                if present(it, 2) and at == 3:
                    pe.wait_ge(s_oev, result_index("B", 0, it - 2) + 1)
                    turn("ob", it - 2, OT[2])
                if present(it, 1):
                    b = it - 1
                    if at == 4:
                        ff2(b)
                    if at == 5.5:
                        pe.wait_ge(lnf.done.sem, lnf.done.upto(b, NT))
                        turn("x1T", b, x1)
                    if at == 6:
                        proj(b)
                    if at == 6.5:
                        logits(b)
                if present(it, -1) and at == 7:
                    turn_part(it + 1, 0)
                if present(it, 2) and at == 7.5:
                    pe.wait_ge(ln_x2.done.sem, ln_x2.done.upto(it - 2, NT))
                    turn("xT2", it - 2, x2)
                if present(it, 0) and at == 8:
                    pe.wait_ge(s_oev, result_index("A", 0, it) + 1)
                    turn("oa0", it, OT[0])
                if present(it, -1) and at in (9, 9.5):
                    turn_part(it + 1, int(2 * at - 17))
                if present(it, 0) and at == 12:
                    pe.wait_ge(s_oev, result_index("A", 1, it) + 1)
                    turn("oa1", it, OT[1])
                if at == int(at):
                    if now:
                        scores(now, 0)
                    if now:
                        scores(now, 1)
                    if back2:
                        transposes(back2, 0)
                    if now:
                        scores(now, 2)
                    if back2:
                        transposes(back2, 1)
                    if back2:
                        transposes(back2, 2)
                    if now:
                        scores(now, 3)
                    if back3:
                        values(back3, 0)
                        values(back3, 1)
                else:
                    if back2:
                        transposes(back2, 3)
            run_iterations(pe, half_slot)

            pe.wait_ge(s_flag, 2)
            pe.wait_ge(s_xfree, len(X_USES) * B)
            pe.matmul(X[0:1, 0:1], fmax[:, :], ones1[:, :], start=True, stop=True).then_inc(s_flag, 1)

            def general_pe(b):
                for k in range(2):
                    n = 2 * b + k
                    xk = x2 if k == 0 else x3
                    if k == 0:
                        pe.wait_ge(s_gload, 16 * 2 * (b + 1))
                    else:
                        pe.wait_ge(ln_g.done.sem, ln_g.done.upto(n - 1, NT))
                    for t in range(NT):
                        ins = pe.transpose(X[:, P * t:P * (t + 1)], xk[:, t, :], identf[:, :])
                    ins.then_inc(g_pe.sem, 1)
                    for i in range(NT):
                        pe.wait_ge(g_dve.sem, g_dve.upto(n, 4 + 12 * i))
                        for m in range(4):
                            ins = pe.matmul(four[m][:, :], Pr[1][:, m, P * i:P * (i + 1)],
                                            xT23[:, :], start=True, stop=True)
                        ins.then_inc(g_pe.sem, 1)
                    pe.wait_ge(g_act.sem, g_act.upto(n, 1 + NT))
                    for i in range(NT):
                        for j in range(NT):
                            ins = pe.transpose(four[i][:, P * j:P * (j + 1)],
                                               Pr[0][:, i, P * j:P * (j + 1)], identf[:, :])
                    ins.then_inc(g_pe.sem, 1)
                    pe.wait_ge(g_act.sem, g_act.upto(n, 1 + 2 * NT))
                    for i in range(NT):
                        for j in range(NT):
                            ins = pe.matmul(O[:, D * i:D * (i + 1)], Y[1][:, i, P * j:P * (j + 1)], xk[:, j, :],
                                            start=(j == 0), stop=(j == NT - 1))
                    ins.then_inc(g_pe.sem, 1)
            general(pe, general_pe)


_INS = ["x", "adj", "L0_gnn_gamma1", "L0_gnn_beta1", "L0_gnn_gamma2", "L0_gnn_beta2", "L0_gnn_W1", "L0_gnn_b1",
        "L0_gnn_W2", "L0_gnn_b2", "L1_gnn_W", "L1_gnn_WT", "L1_gnn_b", "L1_gnn_a",
        "L2_gnn_a0", "L2_gnn_a1", "L2_gnn_a2", "L2_gnn_a3", "L3_gnn_a_0", "L3_gnn_a_1", "L3_gnn_a_2", "L3_gnn_a_3"]


def kernel(**inputs):
    import numpy as _np
    import concourse.bacc as _bacc
    from concourse import mybir as _mybir
    from concourse.bass_utils import run_bass_kernel_spmd as _run

    nc = _bacc.Bacc("TRN2", target_bir_lowering=False, num_devices=1)
    arrays, aps = {}, []
    for name in _INS:
        if name == "L1_gnn_WT":
            a = _np.ascontiguousarray(_np.asarray(inputs["L1_gnn_W"]).T)
        else:
            a = _np.ascontiguousarray(inputs[name])
        if name.startswith(("L2_", "L3_")):
            a = a.reshape(128, 1)
        arrays[f"in_{name}"] = a
        aps.append(nc.dram_tensor(f"in_{name}", a.shape, _mybir.dt.from_np(a.dtype), kind="ExternalInput").ap())
    out = nc.dram_tensor("out", (16, 512, 128), _mybir.dt.float32, kind="ExternalOutput").ap()
    adj_resnorm_kernel(nc, *aps[:14], aps[14:18], aps[18:22], out)
    r = _run(nc, [arrays], core_ids=[0])
    return r.results[0]["out"]
```
